# Optimizing a Trainium2 kernel written in Bass

```python
import numpy as np
import jax
import jax.numpy as jnp

def _softmax(x, axis=-1):
    return jax.nn.softmax(x, axis=axis)

def _gelu(x):
    return jax.nn.gelu(x, approximate=True)

def _silu(x):
    return jax.nn.silu(x)

def _sigmoid(x):
    return jax.nn.sigmoid(x)

def _layernorm(x, axis=-1, eps=1e-05):
    m = jnp.mean(x, axis=axis, keepdims=True)
    v = jnp.var(x, axis=axis, keepdims=True)
    return (x - m) / jnp.sqrt(v + eps)

def _scatter_add(tgt, idx, src, axis=0):
    return tgt.at[idx].add(src)

def _segment_sum(src, seg, n):
    return jax.ops.segment_sum(src, seg, n)
kernel_name = 'mk_prb_d1_jaxref_r4_9d6eb3'

def setup_inputs(seed: int=0):
    np.random.seed(seed)
    _w = jnp.asarray

    def _L0_attn_setup():
        import jax, jax.numpy as jnp
        import numpy as np
        N_HEAD = 16
        MA_K = 0.02
        LEAKY_SLOPE = 0.02
        NEG_INF = -1000000000.0

        def _heads(t, H):
            B, T, C = t.shape
            return t.reshape(B, T, H, C // H).transpose(0, 2, 1, 3)
        key = jax.random.key(seed)
        k1, k2, k3, k4 = jax.random.split(key, 4)
        B, T, C = (2, 512, 256)
        x = jax.random.normal(k1, (B, T, C), dtype=jnp.float32)
        s = 1.0 / np.sqrt(C)
        W_attn = jax.random.normal(k2, (C, 2 * C), dtype=jnp.float32) * s
        W_k2 = jax.random.normal(k3, (C, C), dtype=jnp.float32) * s
        W_proj = jax.random.normal(k4, (C, C), dtype=jnp.float32) * s
        return {'x': x, 'W_attn': W_attn, 'W_k2': W_k2, 'W_proj': W_proj}
    _L0_attn_in = _L0_attn_setup()

    def _L0_ffn_setup():
        import jax, jax.numpy as jnp
        import numpy as np
        DIM = 256

        def _reference_tuple_inner(x, W_r, W_k, W_v, mu_r, mu_k):
            B, T, C = x.shape
            x_prev = jnp.concatenate([jnp.zeros((B, 1, C), x.dtype), x[:, :-1, :]], axis=1)
            xr = mu_r * x + (1.0 - mu_r) * x_prev
            xk = mu_k * x + (1.0 - mu_k) * x_prev
            r = jax.nn.sigmoid(jnp.einsum('btc,dc->btd', xr, W_r))
            k = jnp.einsum('btc,dc->btd', xk, W_k)
            k_act = jnp.square(jax.nn.relu(k))
            out = r * jnp.einsum('btc,dc->btd', k_act, W_v)
            new_state = x[:, -1, :]
            return (out, new_state)
        key = jax.random.key(seed)
        ks = jax.random.split(key, 6)
        B, T, C = (8, 512, DIM)
        x = jax.random.normal(ks[0], (B, T, C), dtype=jnp.float32)
        s = 1.0 / np.sqrt(C)
        W_r = jax.random.uniform(ks[1], (C, C), jnp.float32, -s, s)
        W_k = jax.random.uniform(ks[2], (C, C), jnp.float32, -s, s)
        W_v = jax.random.uniform(ks[3], (C, C), jnp.float32, -s, s)
        mu_r = jax.random.uniform(ks[4], (C,), jnp.float32)
        mu_k = jax.random.uniform(ks[5], (C,), jnp.float32)
        return {'x': x, 'W_r': W_r, 'W_k': W_k, 'W_v': W_v, 'mu_r': mu_r, 'mu_k': mu_k}
    _L0_ffn_in = _L0_ffn_setup()
    _d = {'L0_attn_x': _L0_attn_in['x'], 'L0_attn_W_attn': _L0_attn_in['W_attn'], 'L0_attn_W_k2': _L0_attn_in['W_k2'], 'L0_attn_W_proj': _L0_attn_in['W_proj'], 'L0_ffn_W_r': _L0_ffn_in['W_r'], 'L0_ffn_W_k': _L0_ffn_in['W_k'], 'L0_ffn_W_v': _L0_ffn_in['W_v'], 'L0_ffn_mu_r': _L0_ffn_in['mu_r'], 'L0_ffn_mu_k': _L0_ffn_in['mu_k']}
    _x0 = _d['L0_attn_x']
    _d['L0_attn_x'] = jax.random.normal(jax.random.fold_in(jax.random.key(seed), 1), (4, 2048, 256), dtype=_x0.dtype)
    del _x0
    return _d

def reference(L0_attn_x, L0_attn_W_attn, L0_attn_W_k2, L0_attn_W_proj, L0_ffn_W_r, L0_ffn_W_k, L0_ffn_W_v, L0_ffn_mu_r, L0_ffn_mu_k):

    def _L0_attn_ref(x, W_attn, W_k2, W_proj):
        import jax, jax.numpy as jnp
        import numpy as np
        N_HEAD = 16
        MA_K = 0.02
        LEAKY_SLOPE = 0.02
        NEG_INF = -1000000000.0

        def _heads(t, H):
            B, T, C = t.shape
            return t.reshape(B, T, H, C // H).transpose(0, 2, 1, 3)
        B, T, C = x.shape
        H = N_HEAD
        d = C // H
        scale = 1.0 / jnp.sqrt(jnp.asarray(d, x.dtype))
        qk = x @ W_attn
        q, k = jnp.split(qk, 2, axis=-1)
        q = _heads(q, H)
        k = _heads(k, H)
        v = _heads(x, H)
        scores = jnp.einsum('bhtd,bhsd->bhts', q, k) * scale
        causal = jnp.tril(jnp.ones((T, T), dtype=bool))
        scores = jnp.where(causal, scores, NEG_INF)
        attn = jax.nn.softmax(scores, axis=-1)
        y = jnp.einsum('bhts,bhsd->bhtd', attn, v)
        e = v[:, :, 1:, :] - y[:, :, :-1, :]
        k2 = _heads(x[:, :-1, :] @ W_k2, H)
        q2 = q[:, :, 1:, :]
        qa = -jax.nn.leaky_relu(-q2 * scale, negative_slope=LEAKY_SLOPE)
        ka = jax.nn.sigmoid(MA_K * (k2 * scale))
        w = jnp.einsum('bhtd,bhsd->bhts', qa, ka)
        w = jnp.tril(w)
        y2 = jnp.einsum('bhts,bhsd->bhtd', w, e)
        y2 = jnp.concatenate([jnp.zeros_like(y2[:, :, :1, :]), y2], axis=2)

        def merge(t):
            return t.transpose(0, 2, 1, 3).reshape(B, T, C)
        return merge(y) @ W_proj + merge(y2) @ W_proj

    def _L0_ffn_ref(x, W_r, W_k, W_v, mu_r, mu_k):
        import jax, jax.numpy as jnp
        import numpy as np
        DIM = 256

        def _reference_tuple_inner(x, W_r, W_k, W_v, mu_r, mu_k):
            B, T, C = x.shape
            x_prev = jnp.concatenate([jnp.zeros((B, 1, C), x.dtype), x[:, :-1, :]], axis=1)
            xr = mu_r * x + (1.0 - mu_r) * x_prev
            xk = mu_k * x + (1.0 - mu_k) * x_prev
            r = jax.nn.sigmoid(jnp.einsum('btc,dc->btd', xr, W_r))
            k = jnp.einsum('btc,dc->btd', xk, W_k)
            k_act = jnp.square(jax.nn.relu(k))
            out = r * jnp.einsum('btc,dc->btd', k_act, W_v)
            new_state = x[:, -1, :]
            return (out, new_state)
        return _reference_tuple_inner(x, W_r, W_k, W_v, mu_r, mu_k)[0]
    x = L0_attn_x
    xn = _layernorm(x, axis=-1)
    x = x + _L0_attn_ref(xn, L0_attn_W_attn, L0_attn_W_k2, L0_attn_W_proj) + _L0_ffn_ref(xn, L0_ffn_W_r, L0_ffn_W_k, L0_ffn_W_v, L0_ffn_mu_r, L0_ffn_mu_k)
    return x

_drawn_inputs = setup_inputs


def setup_inputs(seed=0):
    import zlib

    import numpy as np

    out = dict(_drawn_inputs(seed))
    spreads = {}
    factors = {'L0_attn_W_k2': 64.0,
     'L0_ffn_W_r': 8.0,
     'L0_ffn_W_k': 8.0,
     'L0_ffn_W_v': 8.0,
     'L0_ffn_mu_r': 8.0,
     'L0_ffn_mu_k': 8.0,
     'L0_attn_W_attn': 8.0,
     'L0_attn_W_proj': 6.532}
    for name, (base, spread) in spreads.items():
        noise = np.random.default_rng([zlib.crc32(name.encode()), seed]).standard_normal(out[name].shape)
        drawn = base * np.exp(spread * noise) if base else spread * noise
        out[name] = jnp.asarray(drawn.astype(out[name].dtype))
    for name, factor in factors.items():
        out[name] = (out[name] * factor).astype(out[name].dtype)
    return out
```

```python
import concourse.bass as bass
from concourse import mybir
from contextlib import ExitStack

FP32 = mybir.dt.float32
BF16 = mybir.dt.bfloat16
ALU = mybir.AluOpType
ACT = mybir.ActivationFunctionType
AX = mybir.AxisListType

B, T, C = 4, 2048, 256
H = 16
D = C // H
P = 128
CB = C // P
CH = 512
NTILE = B * T // P
TPC = CH // P
CPB = T // CH
TPB = T // P
QH = 4
QPB = H // QH
NQ = B * QPB
PAD = 32
NS = 3
SCALE = 1.0 / float(D) ** 0.5
MA_K, SLOPE, EPS = 0.02, 0.02, 1e-5
MASKED = -1.0e30
Q_PARTS = (0, 1, 2, 0, 1, 0)
K_PARTS = (0, 0, 0, 1, 1, 2)
SR = D * len(Q_PARTS)
MR = SR + NS


START = 16


def at(i, count=1):
    return slice(i, i + count) if isinstance(i, int) else bass.ds(i, count)


class Scratch:

    def __init__(self, nc):
        def dram(name, shape, dt):
            return nc.dram_tensor(name, shape, dt, kind="Internal").ap()
        self.xn = dram("xn_scratch", [B * T + 1, C], FP32)
        self.v = dram("v_scratch", [NQ, T, QH * PAD], FP32)
        self.q = dram("q_scratch", [NQ, NS, QH * D, T], BF16)
        self.k = dram("k_scratch", [NQ, NS, QH * D, T], BF16)
        self.qa = dram("qa_scratch", [B, CB, P, T], FP32)
        self.ka = dram("ka_scratch", [B * T, C], FP32)
        self.res = dram("res_scratch", [B * T, C], FP32)
        self.y = dram("y_scratch", [NQ, P, T], FP32)


def project_stage(nc, ap, scr):
    with ExitStack() as ctx:
        def sb(name, shape, dt=FP32):
            return ctx.enter_context(nc.sbuf_tensor(name, shape, dt))

        def sem(name):
            return ctx.enter_context(nc.semaphore(name))

        x_all = sb("x_all", [P, NTILE, C])
        stats = sb("stats", [P, NTILE, 6])
        mv = sb("mv", [P, NTILE, 2])
        var = sb("var", [P, NTILE])
        std = sb("std", [P, NTILE])
        inv = sb("inv", [P, NTILE])
        t1 = sb("t1", [P, NTILE])
        t2 = sb("t2", [P, NTILE])
        rstd = sb("rstd", [P, NTILE])
        w_attn = sb("w_attn", [P, CB, 2 * C])
        w_k2 = sb("w_k2", [P, CB, C])
        w_ffn = [sb(f"w_ffn{i}", [P, CB, C]) for i in range(3)]
        w_ffn_t = [sb(f"w_ffn_t{i}", [P, CB, C]) for i in range(3)]
        mu = sb("mu", [P, 2, CB])
        eps = sb("eps", [P, 1])
        zrow = sb("zrow", [1, C])
        ident = sb("p_ident", [P, P])
        xn = [sb(f"xn{i}", [P, TPC, C]) for i in range(2)]
        vpad = [sb(f"vpad{i}", [P, TPC, H, PAD]) for i in range(2)]
        xnt = [sb(f"xnt{i}", [P, CB, CH + 1]) for i in range(2)]
        diff = sb("diff", [P, CB, CH])
        xr = sb("xr", [P, CB, CH])
        xk = sb("xk", [P, CB, CH])
        part = sb("part", [P, 4, NS, CH], BF16)
        rest = [sb(f"rest{i}", [P, CH]) for i in range(2)]
        qan = sb("qan", [P, CB, CH])
        ka = sb("ka", [P, TPC, C])
        rgate = sb("rgate", [P, TPC, C])
        krelu = sb("krelu", [P, CB, CH])
        kact = sb("kact", [P, CB, CH])
        res = sb("res", [P, TPC, C])
        bank = [ctx.enter_context(nc.psum_tensor(f"pbank{i}", [P, CH], FP32)) for i in range(8)]

        x_loaded = [sem(f"x_loaded{b}") for b in range(B)]
        w_loaded = sem("w_loaded")
        consts = sem("p_consts")
        zeroed = sem("p_zeroed")
        wt_done = sem("wt_done")
        wt_copied = sem("wt_copied")
        stat_done = sem("stat_done")
        mv_done = sem("mv_done")
        chain = sem("rstd_chain")
        std_done = sem("std_done")
        tail_stored = sem("tail_stored")
        loop_sems = []

        def loop_sem(name):
            loop_sems.append(sem(name))
            return loop_sems[-1]

        xn_done = loop_sem("xn_done")
        vpad_done = loop_sem("vpad_done")
        xt_done = loop_sem("xt_done")
        xnt_copied = loop_sem("xnt_copied")
        edge_done = loop_sem("edge_done")
        diff_done = loop_sem("diff_done")
        mixed = loop_sem("mixed")
        qk_done = loop_sem("qk_done")
        hi_done = loop_sem("hi_done")
        rest_done = loop_sem("rest_done")
        mid_done = loop_sem("mid_done")
        low_done = loop_sem("low_done")
        slope_done = loop_sem("slope_done")
        qan_done = loop_sem("qan_done")
        k2_done = loop_sem("k2_done")
        ka_done = loop_sem("ka_done")
        kt_done = loop_sem("kt_done")
        relu_done = loop_sem("relu_done")
        kact_done = loop_sem("kact_done")
        r_done = loop_sem("r_done")
        gate_done = loop_sem("gate_done")
        v_done = loop_sem("v_done")
        rv_done = loop_sem("rv_done")
        res_done = loop_sem("res_done")
        xn_stored = [loop_sem(f"xn_stored{i}") for i in range(2)]
        v_stored = [loop_sem(f"v_stored{i}") for i in range(2)]
        part_stored = loop_sem("part_stored")
        qan_stored = loop_sem("qan_stored")
        ka_stored = loop_sem("ka_stored")
        res_stored = loop_sem("res_stored")
        gate = sem("p_gate")
        NC = B * CPB

        x_rows = ap["x"].rearrange("b (n p) c -> p (b n) c", p=P)

        with nc.Block() as block:
            @block.sync
            def _(sp):
                for s in loop_sems:
                    sp.sem_inc(s, START)
                for b in range(B):
                    sp.dma_start(x_all[:, TPB * b:TPB * (b + 1), :],
                                 x_rows[:, TPB * b:TPB * (b + 1), :]).then_inc(x_loaded[b], 16)
                sp.wait_ge(zeroed, 1)
                sp.dma_start(scr.xn[B * T:B * T + 1, :], zrow[:, :]).then_inc(tail_stored, 16)
                sp.wait_ge(tail_stored, 16)

            @block.gpsimd
            def _(pool):
                nc.gpsimd.memset(zrow[:, :], 0.0).then_inc(zeroed, 1)
                nc.gpsimd.memset(ident[:, :], 0.0).then_inc(consts, 1)
                nc.gpsimd.memset(eps[:, :], EPS).then_inc(consts, 1)
                for i in range(2):
                    nc.gpsimd.memset(vpad[i][:, :, :, :], 0.0).then_inc(consts, 1)
                pool.wait_ge(consts, 4)
                nc.gpsimd.affine_select(out=ident[:, :], in_=ident[:, :], compare_op=ALU.not_equal, fill=1.0,
                                        base=0, pattern=[[-1, P]], channel_multiplier=1).then_inc(consts, 1)
                for i in range(2):
                    nc.gpsimd.memset(vpad[i][:, :, :, D:D + 1], 1.0).then_inc(consts, 1)

            @block.scalar
            def _(act):
                act.dma_start(w_attn[:, :, :], ap["w_attn"].rearrange("(k p) n -> p k n", p=P)).then_inc(w_loaded, 16)
                act.dma_start(w_k2[:, :, :], ap["w_k2"].rearrange("(k p) n -> p k n", p=P)).then_inc(w_loaded, 16)
                for i, name in enumerate(("w_r", "w_k", "w_v")):
                    act.dma_start(w_ffn[i][:, :, :],
                                  ap[name].rearrange("(k p) n -> p k n", p=P)).then_inc(w_loaded, 16)
                with nc.allow_non_contiguous_dma(reason="256 mixing weights, one per partition"):
                    for i, name in enumerate(("mu_r", "mu_k")):
                        act.dma_start(mu[:, i, :], ap[name].rearrange("(k p) -> p k", p=P)).then_inc(w_loaded, 16)
                for i in range(3):
                    for k in range(CB):
                        act.wait_ge(wt_done, CB * i + k + 1)
                        nc.scalar.activation(w_ffn_t[i][:, k, :], bank[CB * i + k][:, 0:C],
                                             ACT.Copy).then_inc(wt_copied, 1)
                act.wait_ge(mv_done, NTILE)
                act.wait_ge(consts, 5)
                nc.scalar.activation(std[:, :], mv[:, :, 1], ACT.Sqrt, bias=eps[:, :]).then_inc(std_done, 1)
                act.wait_ge(w_loaded, 16 * 7)

            @block.tensor
            def _(pe):
                pe.wait_ge(w_loaded, 16 * 7)
                pe.wait_ge(consts, 5)
                for i in range(3):
                    for k in range(CB):
                        for m in range(CB):
                            last = nc.tensor.transpose(bank[CB * i + k][:, P * m:P * (m + 1)],
                                                       w_ffn[i][:, m, P * k:P * (k + 1)], ident[:, :])
                        last.then_inc(wt_done, 1)

            @block.vector
            def _(dve):
                for b in range(B):
                    dve.wait_ge(x_loaded[b], 16)
                    for n in range(TPB * b, TPB * (b + 1)):
                        nc.vector.bn_stats(stats[:, n, :], x_all[:, n, :]).then_inc(stat_done, 1)
                for n in range(NTILE):
                    dve.wait_ge(stat_done, n + 1)
                    nc.vector.bn_aggr(mv[:, n, :], stats[:, n, :]).then_inc(mv_done, 1)
                dve.wait_ge(mv_done, NTILE)
                nc.vector.tensor_scalar(var[:, :], mv[:, :, 1], EPS, None, ALU.add).then_inc(chain, 1)
                dve.wait_ge(std_done, 1)
                nc.vector.reciprocal(inv[:, :], std[:, :]).then_inc(chain, 1)
                dve.wait_ge(chain, 2)
                nc.vector.tensor_tensor(t1[:, :], inv[:, :], inv[:, :], ALU.mult).then_inc(chain, 1)
                dve.wait_ge(chain, 3)
                nc.vector.tensor_tensor(t2[:, :], t1[:, :], var[:, :], ALU.mult).then_inc(chain, 1)
                dve.wait_ge(chain, 4)
                nc.vector.tensor_scalar(t1[:, :], t2[:, :], -0.5, 1.5, ALU.mult, ALU.add).then_inc(chain, 1)
                dve.wait_ge(chain, 5)
                nc.vector.tensor_tensor(rstd[:, :], t1[:, :], inv[:, :], ALU.mult).then_inc(chain, 1)
                dve.wait_ge(chain, 6)

        with nc.Block() as block:
            @block.vector
            def _(dve):
                def normalise(c, tile0):
                    for j in range(TPC):
                        i = at(tile0 + j)
                        nc.vector.tensor_scalar(xn[c % 2][:, j, :], x_all[:, i, :].rearrange("p a c -> p (a c)"),
                                                mv[:, i, 0:1].rearrange("p a c -> p (a c)"), rstd[:, i],
                                                ALU.subtract, ALU.mult).then_inc(xn_done, 1)

                def batch(b, last):
                    for c in range(CPB):
                        n = b * CPB + c
                        cur, prev = xnt[c % 2], xnt[(c + 1) % 2]
                        dve.wait_ge(xnt_copied, START + n * CB + CB)
                        dve.wait_ge(mixed, START + n * 4)
                        if c == 0:
                            nc.vector.memset(cur[:, :, 0:1], 0.0).then_inc(edge_done, 1)
                        else:
                            nc.vector.tensor_copy(cur[:, :, 0:1], prev[:, :, CH:CH + 1]).then_inc(edge_done, 1)
                        dve.wait_ge(edge_done, START + n + 1)
                        nc.vector.tensor_tensor(diff[:, :, :], cur[:, :, 1:CH + 1], cur[:, :, 0:CH],
                                                ALU.subtract).then_inc(diff_done, 1)
                        dve.wait_ge(diff_done, START + n + 1)
                        for use, dst, free in ((1, xk, kt_done), (0, xr, r_done)):
                            dve.wait_ge(free, START + n * 2)
                            for k in range(CB):
                                nc.vector.scalar_tensor_tensor(
                                    out=dst[:, k, :], in0=diff[:, k, :], scalar=mu[:, use, k:k + 1],
                                    in1=cur[:, k, 0:CH], op0=ALU.mult, op1=ALU.add).then_inc(mixed, 1)
                        for m in range(4):
                            dve.wait_ge(hi_done, START + n * 4 + m + 1)
                            dve.wait_ge(low_done, START + n * 4 + m - 1)
                            if m < CB:
                                dve.wait_ge(slope_done, START + n * 2 + m + 1)
                            nc.vector.tensor_tensor(rest[m % 2][:, :], bank[2 + m][:, :], part[:, m, 0, :],
                                                    ALU.subtract).then_inc(rest_done, 1)
                            if m < CB:
                                nc.vector.scalar_tensor_tensor(out=qan[:, m, :], in0=bank[2 + m][:, :], scalar=-SCALE,
                                                               in1=qan[:, m, :], op0=ALU.mult,
                                                               op1=ALU.max).then_inc(qan_done, 1)
                        if not (last and c == CPB - 1):
                            dve.wait_ge(xt_done, START + n * CB)
                            dve.wait_ge(vpad_done, START + n)
                            dve.wait_ge(xn_stored[(c + 1) % 2], START + (b * 2 + (c + 1) // 2) * 16)
                            normalise(c + 1, n * TPC + TPC)
                        dve.wait_ge(res_stored, START + n * 16)
                        for u in range(2):
                            dve.wait_ge(v_done, START + n * 2 + u + 1)
                            dve.wait_ge(gate_done, START + n * 2 + u + 1)
                            gate = rgate[:, 2 * u:2 * u + 2, :].rearrange("p a c -> p (a c)")
                            out = res[:, 2 * u:2 * u + 2, :].rearrange("p a c -> p (a c)")
                            nc.vector.tensor_tensor(out, bank[4 + u][:, :], gate, ALU.mult).then_inc(rv_done, 1)
                            dve.wait_ge(rv_done, START + n * 2 + u + 1)
                            nc.vector.tensor_tensor(
                                out, out, x_all[:, at(n * TPC + 2 * u, 2), :].rearrange("p a c -> p (a c)"),
                                ALU.add).then_inc(res_done, 1)

                normalise(0, 0)
                with dve.Fori(0, B - 1) as b:
                    batch(b, False)
                batch(B - 1, True)

            @block.tensor
            def _(pe):
                def transpose_chunk(c, n):
                    pe.wait_ge(xn_done, START + n * TPC + TPC)
                    pe.wait_ge(relu_done, START + n * 2)
                    for k in range(CB):
                        for j in range(TPC):
                            last = nc.tensor.transpose(bank[k][:, P * j:P * (j + 1)],
                                                       xn[c % 2][:, j, P * k:P * (k + 1)], ident[:, :])
                        last.then_inc(xt_done, 1)

                def batch(b, last_batch):
                    for c in range(CPB):
                        n = b * CPB + c
                        xt = xnt[c % 2]
                        pe.wait_ge(xnt_copied, START + n * CB + CB)
                        for m in range(4):
                            pe.wait_ge(gate_done if m < 2 else rv_done, START + n * 2)
                            for k in range(CB):
                                last = nc.tensor.matmul(bank[2 + m][:, :], w_attn[:, k, P * m:P * (m + 1)],
                                                        xt[:, k, 1:CH + 1], start=(k == 0), stop=(k == CB - 1))
                            last.then_inc(qk_done, 1)
                        pe.wait_ge(ka_done, START + n * 2)
                        for u in range(2):
                            for j in range(2):
                                t0 = 1 + P * (2 * u + j)
                                for k in range(CB):
                                    last = nc.tensor.matmul(bank[6 + u][:, C * j:C * (j + 1)], xt[:, k, t0:t0 + P],
                                                            w_k2[:, k, :], start=(k == 0), stop=(k == CB - 1))
                            last.then_inc(k2_done, 1)
                        pe.wait_ge(mixed, START + n * 4 + 2)
                        for m in range(CB):
                            for k in range(CB):
                                last = nc.tensor.matmul(bank[m][:, :], w_ffn_t[1][:, k, P * m:P * (m + 1)],
                                                        xk[:, k, :], start=(k == 0), stop=(k == CB - 1))
                            last.then_inc(kt_done, 1)
                        pe.wait_ge(mixed, START + n * 4 + 4)
                        pe.wait_ge(rest_done, START + n * 4 + 2)
                        pe.wait_ge(qan_done, START + n * 2 + 2)
                        for u in range(2):
                            for j in range(2):
                                t0 = P * (2 * u + j)
                                for k in range(CB):
                                    last = nc.tensor.matmul(bank[2 + u][:, C * j:C * (j + 1)], xr[:, k, t0:t0 + P],
                                                            w_ffn_t[0][:, k, :], start=(k == 0), stop=(k == CB - 1))
                            last.then_inc(r_done, 1)
                        if not (last_batch and c == CPB - 1):
                            transpose_chunk(c + 1, n + 1)
                        pe.wait_ge(kact_done, START + n * 2 + 2)
                        pe.wait_ge(rest_done, START + n * 4 + 4)
                        for u in range(2):
                            for j in range(2):
                                t0 = P * (2 * u + j)
                                for k in range(CB):
                                    last = nc.tensor.matmul(bank[4 + u][:, C * j:C * (j + 1)], kact[:, k, t0:t0 + P],
                                                            w_ffn_t[2][:, k, :], start=(k == 0), stop=(k == CB - 1))
                            last.then_inc(v_done, 1)

                transpose_chunk(0, 0)
                with pe.Fori(0, B - 1) as b:
                    batch(b, False)
                batch(B - 1, True)

            @block.scalar
            def _(act):
                def copy_xnt(c, n):
                    act.wait_ge(mixed, START + n * 4 - 4)
                    act.wait_ge(edge_done, START + n)
                    for k in range(CB):
                        act.wait_ge(xt_done, START + n * CB + k + 1)
                        nc.scalar.activation(xnt[c % 2][:, k, 1:CH + 1], bank[k][:, :],
                                             ACT.Copy).then_inc(xnt_copied, 1)

                def batch(b, last):
                    for c in range(CPB):
                        n = b * CPB + c
                        act.wait_ge(part_stored, START + n * 16 * 8)
                        act.wait_ge(qan_stored, START + n * 16)
                        for m in range(4):
                            act.wait_ge(qk_done, START + n * 4 + m + 1)
                            nc.scalar.activation(part[:, m, 0, :], bank[2 + m][:, :], ACT.Copy).then_inc(hi_done, 1)
                            if m < CB:
                                nc.scalar.activation(qan[:, m, :], bank[2 + m][:, :], ACT.Copy,
                                                     scale=-SCALE * SLOPE).then_inc(slope_done, 1)
                        act.wait_ge(ka_stored, START + n * 16)
                        for u in range(2):
                            act.wait_ge(k2_done, START + n * 2 + u + 1)
                            nc.scalar.activation(ka[:, 2 * u:2 * u + 2, :].rearrange("p a c -> p (a c)"),
                                                 bank[6 + u][:, :], ACT.Sigmoid,
                                                 scale=MA_K * SCALE).then_inc(ka_done, 1)
                        act.wait_ge(kact_done, START + n * 2)
                        for m in range(CB):
                            act.wait_ge(kt_done, START + n * 2 + m + 1)
                            nc.scalar.activation(krelu[:, m, :], bank[m][:, :], ACT.Relu).then_inc(relu_done, 1)
                        act.wait_ge(rv_done, START + n * 2)
                        for u in range(2):
                            act.wait_ge(r_done, START + n * 2 + u + 1)
                            nc.scalar.activation(rgate[:, 2 * u:2 * u + 2, :].rearrange("p a c -> p (a c)"),
                                                 bank[2 + u][:, :], ACT.Sigmoid).then_inc(gate_done, 1)
                        if not (last and c == CPB - 1):
                            copy_xnt(c + 1, n + 1)

                copy_xnt(0, 0)
                with act.Fori(0, B - 1) as b:
                    batch(b, False)
                batch(B - 1, True)

            @block.gpsimd
            def _(pool):
                with pool.Fori(0, B) as b:
                    for c in range(CPB):
                        n = b * CPB + c
                        pool.wait_ge(xn_done, START + n * TPC + TPC)
                        pool.wait_ge(v_stored[c % 2], START + (b * 2 + c // 2) * 16 * QPB)
                        pool.sem_inc(gate, 1)
                        nc.gpsimd.tensor_copy(vpad[c % 2][:, :, :, 0:D].rearrange("p j h d -> p (j h) d"),
                                              xn[c % 2][:, :, :].rearrange("p j (h d) -> p (j h) d", d=D)
                                              ).then_inc(vpad_done, 1)
                        pool.wait_ge(part_stored, START + n * 16 * 8)
                        for m in range(4):
                            pool.wait_ge(rest_done, START + n * 4 + m + 1)
                            pool.sem_inc(gate, 1)
                            nc.gpsimd.tensor_copy(part[:, m, 1, :], rest[m % 2][:, :]).then_inc(mid_done, 1)
                            pool.wait_ge(mid_done, START + n * 4 + m + 1)
                            nc.gpsimd.tensor_tensor(part[:, m, 2, :], rest[m % 2][:, :], part[:, m, 1, :],
                                                    ALU.subtract).then_inc(low_done, 1)
                        pool.wait_ge(v_done, START + n * 2)
                        for m in range(CB):
                            pool.wait_ge(relu_done, START + n * 2 + m + 1)
                            nc.gpsimd.tensor_tensor(kact[:, m, :], krelu[:, m, :], krelu[:, m, :],
                                                    ALU.mult).then_inc(kact_done, 1)

            @block.sync
            def _(sp):
                def rows(dram, n):
                    return dram[at(n * CH, CH), :].rearrange("(j p) c -> p j c", p=P)

                with sp.Fori(0, B) as b:
                    for c in range(CPB):
                        n = b * CPB + c
                        ts = slice(CH * c, CH * (c + 1))
                        sp.wait_ge(xn_done, START + n * TPC + TPC)
                        sp.dma_start(rows(scr.xn, n), xn[c % 2][:, :, :]).then_inc(xn_stored[c % 2], 16)
                        sp.wait_ge(vpad_done, START + n + 1)
                        for qd in range(QPB):
                            sp.dma_start(scr.v[at(b * QPB + qd), ts, :].rearrange("a (j p) w -> p (a j) w", p=P),
                                         vpad[c % 2][:, :, QH * qd:QH * (qd + 1), :].rearrange("p j h w -> p j (h w)")
                                         ).then_inc(v_stored[c % 2], 16)
                        sp.wait_ge(qan_done, START + n * 2 + 2)
                        sp.dma_start(scr.qa[at(b), :, :, ts].rearrange("a k p t -> p (a k) t"),
                                     qan[:, :, :]).then_inc(qan_stored, 16)
                        for m in range(4):
                            sp.wait_ge(low_done, START + n * 4 + m + 1)
                            dst = scr.q if m < 2 else scr.k
                            for half in range(2):
                                sp.dma_start(
                                    dst[at(b * QPB + 2 * (m % 2) + half), :, :, ts].rearrange("a s r t -> (a r) s t"),
                                    part[64 * half:64 * half + 64, m, :, :]).then_inc(part_stored, 16)
                        sp.wait_ge(ka_done, START + n * 2 + 2)
                        sp.dma_start(rows(scr.ka, n), ka[:, :, :]).then_inc(ka_stored, 16)
                        sp.wait_ge(res_done, START + n * 2 + 2)
                        sp.dma_start(rows(scr.res, n), res[:, :, :]).then_inc(res_stored, 16)
                for i in range(2):
                    sp.wait_ge(xn_stored[i], START + NC // 2 * 16)
                    sp.wait_ge(v_stored[i], START + NC // 2 * 16 * QPB)
                sp.wait_ge(part_stored, START + NC * 16 * 8)
                sp.wait_ge(qan_stored, START + NC * 16)
                sp.wait_ge(ka_stored, START + NC * 16)
                sp.wait_ge(res_stored, START + NC * 16)


def attention_stage(nc, scr):
    NK = T // P
    BUFS = 3
    SLOTS = 3
    PAIRS = 3
    RQ = 6
    VQ = 2
    SEGS = CPB
    units = [(i, h, seg) for i in range(NK) for h in range(QH) for seg in range(i // TPC + 1)]
    NU = len(units) + 1
    blocks = [(c, j) for c in range(CPB) for j in range(TPC * (c + 1))]
    NB = len(blocks)
    assert BUFS * NU % SLOTS == 0 and BUFS * NB % PAIRS == 0 and (NQ - 1) % BUFS == 0

    def cut(c, j):
        return max(0, P * (j - TPC * c))

    def width(u):
        i, _, seg = u
        return min(CH, P * (i + 1) - CH * seg)

    cost = [sum(CH - cut(*blk) for blk in blocks[:n + 1]) for n in range(NB)]
    ucost = [sum(width(u) for u in units[:n + 1]) for n in range(len(units))]
    LEAD = 0.90
    quota = [sum(uc <= ucost[-1] * co / (LEAD * cost[-1]) for uc in ucost) for co in cost]
    quota = [min(q, len(units)) for q in quota]
    full = quota.index(len(units))
    turn_at = min(full + 2, NB - 1)

    with ExitStack() as ctx:
        def sb(name, shape, dt=FP32):
            return ctx.enter_context(nc.sbuf_tensor(name, shape, dt))

        def sem(name):
            return ctx.enter_context(nc.semaphore(name))

        qst = [sb(f"qst{i}", [P, QH, T], BF16) for i in range(BUFS)]
        kst = [sb(f"kst{i}", [P, QH, T], BF16) for i in range(BUFS)]
        val = [sb(f"val{i}", [P, NK, QH * PAD]) for i in range(BUFS)]
        prob = [sb(f"prob{i}", [P, 2, CH]) for i in range(2 * PAIRS)]
        yt = [sb(f"yt{i}", [P, CH]) for i in range(2)]
        pmax = sb("pmax", [P, NK * QH, SEGS])
        nmax = sb("nmax", [P, NK * QH])
        nrest = sb("nrest", [P, NK * QH])
        npart = sb("npart", [P, NS, NK * QH], BF16)
        mrow = sb("mrow", [NK * QH, NS, P], BF16)
        ident = sb("a_ident", [P, P], BF16)
        mask_kq = sb("mask_kq", [P, P], BF16)
        mask_qk = sb("mask_qk", [P, P], BF16)
        score = [ctx.enter_context(nc.psum_tensor(f"score{i}", [P, 2, CH], FP32)) for i in range(2)]
        acc = ctx.enter_context(nc.psum_tensor("acc", [P, CH], FP32))
        slot = [ctx.enter_context(nc.psum_tensor(f"slot{i}", [P, CH], FP32)) for i in range(SLOTS)]

        consts = sem("a_consts")
        loop_sems = []

        def loop_sem(name):
            loop_sems.append(sem(name))
            return loop_sems[-1]

        q_loaded = [loop_sem(f"q_loaded{i}") for i in range(BUFS)]
        v_loaded = [loop_sem(f"v_loaded{i}") for i in range(BUFS)]
        m_loaded = [loop_sem(f"m_loaded{i}") for i in range(BUFS)]
        peak_scored = loop_sem("peak_scored")
        peak_read = loop_sem("peak_read")
        nmax_done = loop_sem("nmax_done")
        scored = loop_sem("scored")
        exp_done = loop_sem("exp_done")
        pv_done = loop_sem("pv_done")
        acc_copied = loop_sem("acc_copied")
        gate = sem("a_gate")
        y_stored = [loop_sem(f"y_stored{i}") for i in range(2)]

        with nc.Block() as block:
            @block.sync
            def _(sp):
                for s in loop_sems:
                    sp.sem_inc(s, START)

            @block.vector
            def _(dve):
                nc.vector.memset(pmax[:, :, :], -3.0e38).then_inc(consts, 1)
                for i in range(BUFS):
                    nc.vector.memset(kst[i][SR:MR, :, :], 1.0).then_inc(consts, 1)

            @block.gpsimd
            def _(pool):
                nc.gpsimd.memset(ident[:, :], 0.0).then_inc(consts, 1)
                nc.gpsimd.memset(mask_kq[:, :], 0.0).then_inc(consts, 1)
                nc.gpsimd.memset(mask_qk[:, :], 0.0).then_inc(consts, 1)
                pool.wait_ge(consts, BUFS + 4)
                nc.gpsimd.affine_select(out=ident[:, :], in_=ident[:, :], compare_op=ALU.not_equal, fill=1.0,
                                        base=0, pattern=[[-1, P]], channel_multiplier=1).then_inc(consts, 1)
                nc.gpsimd.affine_select(out=mask_kq[:, :], in_=mask_kq[:, :], compare_op=ALU.is_ge, fill=MASKED,
                                        base=0, pattern=[[1, P]], channel_multiplier=-1).then_inc(consts, 1)
                nc.gpsimd.affine_select(out=mask_qk[:, :], in_=mask_qk[:, :], compare_op=ALU.is_ge, fill=MASKED,
                                        base=0, pattern=[[-1, P]], channel_multiplier=1).then_inc(consts, 1)

        def steps(eng, step):
            step(0, 0, True, False)
            with eng.Fori(0, (NQ - 1) // BUFS) as r:
                for s in range(1, BUFS + 1):
                    step(r, s, True, True)
            step(NQ // BUFS, NQ % BUFS, False, True)

        def filled(r, s):
            return r + s // BUFS + 1

        with nc.Block() as block:
            @block.sync
            def _(sp):
                def load(n, buf):
                    for i, part in enumerate(Q_PARTS):
                        sp.dma_start(qst[buf][D * i:D * (i + 1), :, :],
                                     scr.q[at(n), part, :, :].rearrange("a (h d) t -> d (a h) t", d=D)
                                     ).then_inc(q_loaded[buf], 16)
                    for i, part in enumerate(K_PARTS):
                        sp.dma_start(kst[buf][D * i:D * (i + 1), :, :],
                                     scr.k[at(n), part, :, :].rearrange("a (h d) t -> d (a h) t", d=D)
                                     ).then_inc(q_loaded[buf], 16)
                    for i in range(VQ):
                        some = slice(NK // VQ * i, NK // VQ * (i + 1))
                        sp.dma_start(val[buf][:, some, :],
                                     scr.v[at(n), :, :].rearrange("a (j p) w -> p (a j) w", p=P)[:, some, :]
                                     ).then_inc(v_loaded[buf], 16)

                def store(n, c):
                    sp.wait_ge(acc_copied, START + (n - 1) * CPB + c + 1)
                    sp.dma_start(scr.y[at(n - 1), :, CH * c:CH * (c + 1)].rearrange("a p t -> (a p) t"),
                                 yt[c % 2][:, :]).then_inc(y_stored[c % 2], 16)

                def rows(n, buf):
                    sp.wait_ge(peak_read, START + n * NU + NU)
                    for i in range(NS):
                        sp.dma_start(qst[buf][SR + i:SR + i + 1, :, :].rearrange("a h (i t) -> a (h i) t", t=P),
                                     mrow[:, i, :]).then_inc(m_loaded[buf], 16)

                def step(r, s, more):
                    n = r * BUFS + s
                    sp.wait_ge(pv_done, START + (n - 1) * NB)
                    if more:
                        load(n + 1, (s + 1) % BUFS)
                    for c in range(CPB - 1):
                        store(n, c)
                    rows(n, s % BUFS)
                    store(n, CPB - 1)

                load(0, 0)
                load(1, 1)
                rows(0, 0)
                with sp.Fori(0, (NQ - 1) // BUFS - 1) as r:
                    for s in range(1, BUFS + 1):
                        step(r, s, True)
                for s in range(1, BUFS + 1):
                    step((NQ - 1) // BUFS - 1, s, s < BUFS)
                for c in range(CPB):
                    store(NQ, c)
                for i in range(2):
                    sp.wait_ge(y_stored[i], START + NQ * CPB // 2 * 16)

            @block.tensor
            def _(pe):
                def peak(r, s, w):
                    n = r * BUFS + s
                    buf, dst = s % BUFS, slot[(NU * s + w) % SLOTS]
                    i, h, seg = units[w]
                    wd = width(units[w])
                    diag = seg == i // TPC
                    pe.wait_ge(peak_read, START + n * NU + w - SLOTS + 1)
                    last = nc.tensor.matmul(dst[:, 0:wd], qst[buf][0:SR, h, P * i:P * (i + 1)],
                                            kst[buf][0:SR, h, CH * seg:CH * seg + wd], start=True, stop=not diag)
                    if diag:
                        last = nc.tensor.matmul(dst[:, wd - P:wd], ident[:, :], mask_qk[:, :], start=False, stop=True)
                    last.then_inc(peak_scored, 1)

                def turn(r, s):
                    n = r * BUFS + s
                    dst = slot[(NU * s + NU - 1) % SLOTS][:, :].bitcast(BF16)
                    pe.wait_ge(peak_read, START + n * NU + NU - SLOTS)
                    pe.wait_ge(nmax_done, START + n * 5 + 5)
                    pe.sem_inc(gate, 1)
                    for i in range(NS):
                        last = nc.tensor.transpose(dst[0:NK * QH, P * i:P * (i + 1)], npart[:, i, :], ident[:, :])
                    last.then_inc(peak_scored, 1)

                def scores(r, s, b, half):
                    m = r * BUFS + s - 1
                    c, j = blocks[b]
                    q, k, dst = qst[(s - 1) % BUFS], kst[(s - 1) % BUFS], score[half]
                    t0 = CH * c + cut(c, j)
                    wd = CH - cut(c, j)
                    diag = j >= TPC * c
                    pe.wait_ge(exp_done, START + m * 2 * NB + 2 * b + half - 1)
                    for e in range(2):
                        h = 2 * half + e
                        last = nc.tensor.matmul(dst[:, e, 0:wd], k[0:MR, h, P * j:P * (j + 1)],
                                                q[0:MR, h, t0:t0 + wd], start=True, stop=not diag)
                        if diag:
                            last = nc.tensor.matmul(dst[:, e, 0:P], ident[:, :], mask_kq[:, :],
                                                    start=False, stop=True)
                    last.then_inc(scored, 1)

                def product(r, s, b):
                    m = r * BUFS + s - 1
                    c, j = blocks[b]
                    v = val[(s - 1) % BUFS]
                    wd = CH - cut(c, j)
                    pe.wait_ge(exp_done, START + m * 2 * NB + 2 * b + 2)
                    if j == 0:
                        pe.wait_ge(acc_copied, START + m * CPB + c)
                    for h in range(QH):
                        p = prob[(2 * (NB * (s - 1) + b) + h // 2) % (2 * PAIRS)]
                        last = nc.tensor.matmul(acc[PAD * h:PAD * (h + 1), cut(c, j):CH],
                                                v[:, j, PAD * h:PAD * (h + 1)], p[:, h % 2, 0:wd],
                                                start=(j == 0), stop=(j == TPC * (c + 1) - 1))
                    last.then_inc(pv_done, 1)

                def step(r, s, peaks, main):
                    if peaks:
                        pe.wait_ge(q_loaded[s % BUFS], START + 16 * 2 * RQ * filled(r, s))
                    if not main:
                        for w in range(len(units)):
                            peak(r, s, w)
                        turn(r, s)
                        return
                    pe.wait_ge(m_loaded[(s - 1) % BUFS], START + 16 * NS * filled(r, s - 1))
                    pe.wait_ge(v_loaded[(s - 1) % BUFS], START + 16 * VQ * filled(r, s - 1))
                    done = 0
                    for b in range(NB):
                        todo = quota[b] - done if peaks else 0
                        gap = [todo // 3 + (todo % 3 > x) for x in range(3)]
                        for x in range(3):
                            if x < 2:
                                scores(r, s, b, x)
                            elif b > 0:
                                product(r, s, b - 1)
                            for _ in range(gap[x]):
                                peak(r, s, done)
                                done += 1
                        if peaks and b == turn_at:
                            turn(r, s)
                    product(r, s, NB - 1)

                pe.wait_ge(consts, BUFS + 7)
                steps(pe, step)

            @block.scalar
            def _(act):
                def step(r, s, peaks, main):
                    if not main:
                        return
                    m = r * BUFS + s - 1
                    for b, (c, j) in enumerate(blocks):
                        wd = CH - cut(c, j)
                        act.wait_ge(pv_done, START + m * NB + b - PAIRS + 1)
                        for half in range(2):
                            p = prob[(2 * (NB * (s - 1) + b) + half) % (2 * PAIRS)]
                            act.wait_ge(scored, START + m * 2 * NB + 2 * b + half + 1)
                            nc.scalar.activation(p[:, :, 0:wd], score[half][:, :, 0:wd], ACT.Exp,
                                                 scale=SCALE).then_inc(exp_done, 1)
                        if c and j == 0:
                            copy_sums(m, c - 1, b)
                    copy_sums(m, CPB - 1, NB)

                def copy_sums(m, c, products):
                    act.wait_ge(pv_done, START + m * NB + products)
                    act.wait_ge(y_stored[c % 2], START + (m * (CPB // 2) + c // 2) * 16)
                    nc.scalar.activation(yt[c % 2][:, :], acc[:, :], ACT.Copy).then_inc(acc_copied, 1)

                steps(act, step)

            @block.vector
            def _(dve):
                def step(r, s, peaks, main):
                    if not peaks:
                        return
                    n = r * BUFS + s
                    for w, u in enumerate(units):
                        i, h, seg = u
                        dve.wait_ge(peak_scored, START + n * NU + w + 1)
                        if w == 0:
                            dve.wait_ge(nmax_done, START + n * 5)
                        nc.vector.tensor_reduce(pmax[:, NK * h + i, seg:seg + 1],
                                                slot[(NU * s + w) % SLOTS][:, 0:width(u)], AX.X,
                                                ALU.max).then_inc(peak_read, 1)
                    dve.wait_ge(peak_read, START + n * NU + NU - 1)
                    nc.vector.tensor_reduce(nmax[:, :], pmax[:, :, :], AX.X, ALU.max, negate=True
                                            ).then_inc(nmax_done, 1)
                    dve.wait_ge(nmax_done, START + n * 5 + 1)
                    nc.vector.tensor_copy(npart[:, 0, :], nmax[:, :]).then_inc(nmax_done, 1)
                    dve.wait_ge(nmax_done, START + n * 5 + 2)
                    nc.vector.tensor_tensor(nrest[:, :], nmax[:, :], npart[:, 0, :], ALU.subtract
                                            ).then_inc(nmax_done, 1)
                    dve.wait_ge(nmax_done, START + n * 5 + 3)
                    nc.vector.tensor_copy(npart[:, 1, :], nrest[:, :]).then_inc(nmax_done, 1)
                    dve.wait_ge(nmax_done, START + n * 5 + 4)
                    nc.vector.tensor_tensor(npart[:, 2, :], nrest[:, :], npart[:, 1, :], ALU.subtract
                                            ).then_inc(nmax_done, 1)
                    dve.wait_ge(peak_scored, START + n * NU + NU)
                    back = (s - 1) % BUFS
                    fills = r + (s - 1) // BUFS + 1
                    dve.wait_ge(m_loaded[back], START + 16 * NS * fills)
                    nc.vector.tensor_copy(mrow[:, :, :].rearrange("p s t -> p (s t)"),
                                          slot[(NU * s + NU - 1) % SLOTS][:, :].bitcast(BF16)[0:NK * QH, 0:NS * P]
                                          ).then_inc(peak_read, 1)

                dve.wait_ge(consts, BUFS + 7)
                steps(dve, step)


def mix_stage(nc, ap, scr):
    TILES = 2
    NI = TILES * B
    STEPS = TPB // TILES
    GH = P // D
    with ExitStack() as ctx:
        def sb(name, shape, dt=FP32):
            return ctx.enter_context(nc.sbuf_tensor(name, shape, dt))

        def sem(name):
            return ctx.enter_context(nc.semaphore(name))

        w_proj = sb("w_proj", [P, CB, C])
        ident = sb("m_ident", [P, P])
        strict = sb("strict", [P, P])
        own = sb("own", [P, H])
        parity = sb("parity", [P, 2])
        yraw = [sb(f"yraw{i}", [P, QPB, P]) for i in range(NI)]
        vnext = [sb(f"vnext{i}", [P, C]) for i in range(NI)]
        qa = [sb(f"qa{i}", [P, CB, P]) for i in range(NI)]
        ka = [sb(f"ka{i}", [P, C]) for i in range(NI)]
        res = [sb(f"mres{i}", [P, C]) for i in range(NI)]
        qsplit = [sb(f"qsplit{i}", [P, CB, 2, P]) for i in range(2)]
        kat = [sb(f"kat{i}", [P, CB, P]) for i in range(2)]
        den = [sb(f"den{i}", [P, H]) for i in range(2)]
        y = [sb(f"y{i}", [P, H, D]) for i in range(2)]
        e = [sb(f"e{i}", [P, C]) for i in range(2)]
        am = [sb(f"am{i}", [P, 4, CB, 2, P]) for i in range(2)]
        state = [sb(f"state{i}", [P, H, PAD]) for i in range(B)]
        snew = [sb(f"snew{i}", [P, H, D]) for i in range(2)]
        y2t = [sb(f"y2t{i}", [P, QPB * P]) for i in range(2)]
        ysum = [sb(f"ysum{i}", [P, H, D]) for i in range(2)]
        ysumt = [sb(f"ysumt{i}", [P, CB, P]) for i in range(2)]
        outt = [sb(f"outt{i}", [P, C]) for i in range(2)]
        abank = [ctx.enter_context(nc.psum_tensor(f"abank{i}", [P, CB, 2, P], FP32)) for i in range(4)]
        ybank = ctx.enter_context(nc.psum_tensor("ybank", [P, CH], FP32))
        zbank = ctx.enter_context(nc.psum_tensor("zbank", [P, CH], FP32))
        obank = ctx.enter_context(nc.psum_tensor("obank", [P, QPB, P], FP32))
        kbank = ctx.enter_context(nc.psum_tensor("kbank", [P, CH], FP32))

        consts = sem("m_consts")
        w_loaded = sem("m_w_loaded")
        loop_sems = []

        def loop_sem(name):
            loop_sems.append(sem(name))
            return loop_sems[-1]

        loaded = [loop_sem(f"m_loaded{i}") for i in range(NI)]
        yt_done = loop_sem("m_yt")
        den_done = loop_sem("m_den")
        y_done = loop_sem("m_y")
        e_done = loop_sem("m_e")
        kt_done = loop_sem("m_kt")
        kat_done = loop_sem("m_kat")
        split_done = loop_sem("m_split")
        a_done = loop_sem("m_a")
        am_done = loop_sem("m_am")
        o_done = loop_sem("m_o")
        y2t_done = loop_sem("m_y2t")
        s_done = loop_sem("m_s")
        snew_done = loop_sem("m_snew")
        state_done = loop_sem("m_state")
        z_done = loop_sem("m_z")
        ysum_done = loop_sem("m_ysum")
        w_done = loop_sem("m_w")
        ysumt_done = loop_sem("m_ysumt")
        p_done = loop_sem("m_p")
        out_done = loop_sem("m_out")
        gate = sem("m_gate")
        stored = [loop_sem(f"m_stored{i}") for i in range(2)]

        with nc.Block() as block:
            @block.sync
            def _(sp):
                for s in loop_sems:
                    sp.sem_inc(s, START)
                sp.dma_start(w_proj[:, :, :], ap["w_proj"].rearrange("(k p) n -> p k n", p=P)).then_inc(w_loaded, 16)
                sp.wait_ge(w_loaded, 16)

            @block.vector
            def _(dve):
                for b in range(B):
                    nc.vector.memset(state[b][:, :, :], 0.0).then_inc(consts, 1)
                dve.wait_ge(consts, B + 7)
                for i in range(2):
                    nc.vector.tensor_reduce(parity[:, i:i + 1],
                                            own[:, 0:GH].rearrange("p (g i) -> p i g", i=2)[:, i, :],
                                            AX.X, ALU.add).then_inc(consts, 1)

            @block.gpsimd
            def _(pool):
                nc.gpsimd.memset(ident[:, :], 0.0).then_inc(consts, 1)
                nc.gpsimd.memset(strict[:, :], 1.0).then_inc(consts, 1)
                nc.gpsimd.memset(own[:, :], 1.0).then_inc(consts, 1)
                pool.wait_ge(consts, B + 3)
                nc.gpsimd.affine_select(out=ident[:, :], in_=ident[:, :], compare_op=ALU.not_equal, fill=1.0,
                                        base=0, pattern=[[-1, P]], channel_multiplier=1).then_inc(consts, 1)
                nc.gpsimd.affine_select(out=strict[:, :], in_=strict[:, :], compare_op=ALU.is_gt, fill=0.0,
                                        base=0, pattern=[[1, P]], channel_multiplier=-1).then_inc(consts, 1)
                rows = own[:, :].rearrange("p (g h) -> p g h", g=CB)
                nc.gpsimd.affine_select(out=rows, in_=rows, compare_op=ALU.is_ge, fill=0.0,
                                        base=0, pattern=[[0, CB], [-D, GH]], channel_multiplier=1).then_inc(consts, 1)
                pool.wait_ge(consts, B + 6)
                nc.gpsimd.affine_select(out=rows, in_=rows, compare_op=ALU.is_ge, fill=0.0,
                                        base=D - 1, pattern=[[0, CB], [D, GH]],
                                        channel_multiplier=-1).then_inc(consts, 1)

        with nc.Block() as block:
            @block.sync
            def _(sp):
                def load(r, k):
                    b = k % B
                    i = r * TILES + k // B
                    row = i * P + b * T
                    sp.dma_start(yraw[k][:, :, :],
                                 scr.y[QPB * b:QPB * (b + 1), :, at(i * P, P)].rearrange("q p t -> p q t")
                                 ).then_inc(loaded[k], 16)
                    sp.dma_start(ka[k][:, :], scr.ka[at(row, P), :]).then_inc(loaded[k], 16)
                    sp.dma_start(qa[k][:, :, :],
                                 scr.qa[b, :, :, at(i * P, P)].rearrange("k p t -> p k t")).then_inc(loaded[k], 16)
                    sp.dma_start(vnext[k][:, :], scr.xn[at(row + 1, P), :]).then_inc(loaded[k], 16)
                    sp.dma_start(res[k][:, :], scr.res[at(row, P), :]).then_inc(loaded[k], 16)

                def store(r, k):
                    m = r * NI + k
                    row = (r * TILES + k // B) * P
                    sp.wait_ge(out_done, START + m + 1)
                    sp.dma_start(ap["out"][k % B, at(row, P), :], outt[k % 2][:, :]).then_inc(stored[k % 2], 16)

                for k in range(NI):
                    load(0, k)
                with sp.Fori(0, STEPS - 1) as r:
                    for k in range(NI):
                        store(r, k)
                        load(r + 1, k)
                for k in range(NI):
                    store(STEPS - 1, k)
                for i in range(2):
                    sp.wait_ge(stored[i], START + STEPS * NI // 2 * 16)

            @block.tensor
            def _(pe):
                def turn(r, k):
                    m = r * NI + k
                    pe.wait_ge(loaded[k], START + r * 80 + 80)
                    pe.wait_ge(out_done, START + m - 1)
                    for q in range(QPB):
                        last = nc.tensor.transpose(ybank[:, P * q:P * (q + 1)], yraw[k][:, q, :], ident[:, :])
                    last.then_inc(yt_done, 1)
                    pe.wait_ge(snew_done, START + m - 1)
                    for g in range(CB):
                        last = nc.tensor.transpose(kbank[:, P * g:P * (g + 1)], ka[k][:, P * g:P * (g + 1)],
                                                   ident[:, :])
                    last.then_inc(kt_done, 1)

                def inner(r, k):
                    m = r * NI + k
                    pe.wait_ge(kat_done, START + m + 1)
                    pe.wait_ge(split_done, START + m * 2 + 2)
                    for a in range(4):
                        pe.wait_ge(am_done, START + m * 4 - 4 + a + 1)
                        rows = slice(PAD * a, PAD * (a + 1))
                        for g in range(CB):
                            last = nc.tensor.matmul(abank[a][:, g, :, :], kat[k % 2][rows, g, :],
                                                    qsplit[k % 2][rows, g, :, :], start=True, stop=True)
                        last.then_inc(a_done, 1)

                def apply(r, k):
                    m = r * NI + k
                    pe.wait_ge(y2t_done, START + m)
                    pe.wait_ge(state_done, START + m - B + 1)
                    for q in range(QPB):
                        nc.tensor.matmul(obank[:, q, :], state[k % B][:, QH * q:QH * (q + 1), :],
                                         qa[k][:, q * QH // GH, :], start=(q == 0), stop=False, skip_group_check=True)
                    pe.wait_ge(e_done, START + m + 1)
                    pe.wait_ge(am_done, START + m * 4 + 4)
                    for q in range(QPB):
                        for h in range(QH * q, QH * (q + 1)):
                            g, a, par = h // GH, h % GH // 2, h % 2
                            j = h % QH
                            last = nc.tensor.matmul(obank[PAD * j:PAD * j + D, q, :],
                                                    e[k % 2][:, D * h:D * (h + 1)], am[k % 2][:, a, g, par, :],
                                                    start=False, stop=True, skip_group_check=True)
                    last.then_inc(o_done, 1)

                def turn_back(r, k):
                    m = r * NI + k
                    pe.wait_ge(y2t_done, START + m + 1)
                    pe.wait_ge(ysumt_done, START + m)
                    for q in range(QPB):
                        last = nc.tensor.transpose(zbank[:, P * q:P * (q + 1)], y2t[k % 2][:, P * q:P * (q + 1)],
                                                   ident[:, :])
                    last.then_inc(z_done, 1)

                def update(r, k, more):
                    m = r * NI + k
                    pe.wait_ge(kat_done, START + m + 1 + more)
                    pe.wait_ge(snew_done, START + m)
                    for g in range(CB):
                        last = nc.tensor.matmul(kbank[:, C + P * g:C + P * (g + 1)], ka[k][:, P * g:P * (g + 1)],
                                                e[k % 2][:, P * g:P * (g + 1)], start=True, stop=True)
                    last.then_inc(s_done, 1)

                def project(r, k, more):
                    m = r * NI + k
                    pe.wait_ge(ysum_done, START + m + 1)
                    for g in range(CB):
                        last = nc.tensor.transpose(
                            zbank[:, P * g:P * (g + 1)],
                            ysum[k % 2][:, GH * g:GH * (g + 1), :].rearrange("p h d -> p (h d)"), ident[:, :])
                    last.then_inc(w_done, 1)
                    pe.wait_ge(ysumt_done, START + m + 1)
                    pe.wait_ge(y_done, START + m + 1 + more)
                    for g in range(CB):
                        last = nc.tensor.matmul(ybank[:, 0:C], ysumt[k % 2][:, g, :], w_proj[:, g, :],
                                                start=(g == 0), stop=(g == CB - 1))
                    last.then_inc(p_done, 1)

                def step(r, last):
                    for k in range(NI):
                        more = not (last and k == NI - 1)
                        r1, k1 = r + (k + 1) // NI, (k + 1) % NI
                        apply(r, k)
                        if more:
                            turn(r1, k1)
                        turn_back(r, k)
                        if more:
                            inner(r1, k1)
                        update(r, k, more)
                        project(r, k, more)

                turn(0, 0)
                inner(0, 0)
                with pe.Fori(0, STEPS - 1) as r:
                    step(r, False)
                step(STEPS - 1, True)

            @block.gpsimd
            def _(pool):
                with pool.Fori(0, STEPS) as r:
                    for k in range(NI):
                        m = r * NI + k
                        pool.wait_ge(loaded[k], START + r * 80 + 80)
                        pool.wait_ge(a_done, START + m * 4 - 4)
                        pool.sem_inc(gate, 1)
                        for i in range(2):
                            nc.gpsimd.tensor_scalar(qsplit[k % 2][:, :, i, :], qa[k][:, :, :], parity[:, i:i + 1],
                                                    None, ALU.mult).then_inc(split_done, 1)

            @block.scalar
            def _(act):
                def turned(r, k):
                    m = r * NI + k
                    act.wait_ge(kt_done, START + m + 1)
                    act.wait_ge(a_done, START + m * 4 - 4)
                    nc.scalar.activation(kat[k % 2][:, :, :].rearrange("p g t -> p (g t)"), kbank[:, 0:C],
                                         ACT.Copy).then_inc(kat_done, 1)

                def back(r, k):
                    m = r * NI + k
                    act.wait_ge(o_done, START + m + 1)
                    act.wait_ge(z_done, START + m - 1)
                    nc.scalar.activation(y2t[k % 2][:, :], obank[:, :, :].rearrange("p q t -> p (q t)"),
                                         ACT.Copy).then_inc(y2t_done, 1)

                def both(r, k):
                    m = r * NI + k
                    act.wait_ge(w_done, START + m + 1)
                    act.wait_ge(p_done, START + m - 1)
                    nc.scalar.activation(ysumt[k % 2][:, :, :].rearrange("p g t -> p (g t)"), zbank[:, 0:C],
                                         ACT.Copy).then_inc(ysumt_done, 1)

                def step(r, last):
                    for k in range(NI):
                        back(r, k)
                        if not (last and k == NI - 1):
                            turned(r + (k + 1) // NI, (k + 1) % NI)
                        both(r, k)

                turned(0, 0)
                with act.Fori(0, STEPS - 1) as r:
                    step(r, False)
                step(STEPS - 1, True)

            @block.vector
            def _(dve):
                def attention(r, k):
                    m = r * NI + k
                    dve.wait_ge(yt_done, START + m + 1)
                    sums = ybank[:, :].rearrange("p (h w) -> p h w", w=PAD)
                    nc.vector.reciprocal(den[k % 2][:, :], sums[:, :, D]).then_inc(den_done, 1)
                    dve.wait_ge(den_done, START + m + 1)
                    dve.wait_ge(ysum_done, START + m - 1)
                    nc.vector.tensor_tensor(y[k % 2][:, :, :], sums[:, :, 0:D],
                                            den[k % 2][:, :].unsqueeze(2).to_broadcast([P, H, D]),
                                            ALU.mult).then_inc(y_done, 1)
                    dve.wait_ge(y_done, START + m + 1)
                    dve.wait_ge(s_done, START + m - 1)
                    nc.vector.tensor_tensor(e[k % 2][:, :], y[k % 2][:, :, :].rearrange("p h d -> p (h d)"),
                                            vnext[k][:, :], ALU.subtract).then_inc(e_done, 1)

                def masks(r, k):
                    m = r * NI + k
                    dve.wait_ge(o_done, START + m - 1)
                    for a in range(4):
                        dve.wait_ge(a_done, START + m * 4 + a + 1)
                        nc.vector.tensor_tensor(am[k % 2][:, a, :, :, :].rearrange("p g i t -> p (g i) t"),
                                                abank[a][:, :, :, :].rearrange("p g i t -> p (g i) t"),
                                                strict[:, :].unsqueeze(1).to_broadcast([P, 2 * CB, P]),
                                                ALU.mult).then_inc(am_done, 1)

                def total(r, k):
                    m = r * NI + k
                    dve.wait_ge(z_done, START + m + 1)
                    dve.wait_ge(w_done, START + m - 1)
                    nc.vector.tensor_tensor(ysum[k % 2][:, :, :],
                                            zbank[:, :].rearrange("p (h w) -> p h w", w=PAD)[:, :, 0:D],
                                            y[k % 2][:, :, :], ALU.add).then_inc(ysum_done, 1)

                def finish(r, k):
                    m = r * NI + k
                    dve.wait_ge(s_done, START + m + 1)
                    nc.vector.tensor_tensor(snew[k % 2][:, :, :],
                                            kbank[:, C:2 * C].rearrange("p (h d) -> p h d", d=D),
                                            own[:, :].unsqueeze(2).to_broadcast([P, H, D]),
                                            ALU.mult).then_inc(snew_done, 1)
                    dve.wait_ge(snew_done, START + m + 1)
                    nc.vector.tensor_tensor(state[k % B][:, :, 0:D], state[k % B][:, :, 0:D], snew[k % 2][:, :, :],
                                            ALU.add).then_inc(state_done, 1)
                    dve.wait_ge(p_done, START + m + 1)
                    dve.wait_ge(stored[k % 2], START + (r * (NI // 2) + k // 2) * 16)
                    nc.vector.tensor_tensor(outt[k % 2][:, :], ybank[:, 0:C], res[k][:, :],
                                            ALU.add).then_inc(out_done, 1)

                def step(r, last):
                    for k in range(NI):
                        more = not (last and k == NI - 1)
                        r1, k1 = r + (k + 1) // NI, (k + 1) % NI
                        if more:
                            attention(r1, k1)
                        total(r, k)
                        if more:
                            masks(r1, k1)
                        finish(r, k)

                attention(0, 0)
                masks(0, 0)
                with dve.Fori(0, STEPS - 1) as r:
                    step(r, False)
                step(STEPS - 1, True)


def build(nc, x, w_attn, w_k2, w_proj, w_r, w_k, w_v, mu_r, mu_k, out):
    ap = dict(x=x, w_attn=w_attn, w_k2=w_k2, w_proj=w_proj, w_r=w_r, w_k=w_k, w_v=w_v,
              mu_r=mu_r, mu_k=mu_k, out=out)
    scr = Scratch(nc)
    project_stage(nc, ap, scr)
    attention_stage(nc, scr)
    mix_stage(nc, ap, scr)


_INS = ['L0_attn_x', 'L0_attn_W_attn', 'L0_attn_W_k2', 'L0_attn_W_proj', 'L0_ffn_W_r', 'L0_ffn_W_k',
        'L0_ffn_W_v', 'L0_ffn_mu_r', 'L0_ffn_mu_k']
_OUTS = [((B, T, C), 'float32')]


def kernel(**inputs):
    import numpy as _np
    import concourse.bacc as _bacc
    from concourse import mybir as _mybir
    from concourse.bass_utils import run_bass_kernel_spmd as _run

    nc = _bacc.Bacc("TRN2", target_bir_lowering=False, num_devices=1)
    arrays, args = {}, []
    for name in _INS:
        a = _np.ascontiguousarray(inputs[name])
        arrays[f"in_{name}_dram"] = a
        args.append(nc.dram_tensor(f"in_{name}_dram", a.shape, _mybir.dt.from_np(a.dtype), kind="ExternalInput").ap())
    for i, (shape, dtype) in enumerate(_OUTS):
        dt = _mybir.dt.from_np(_np.dtype(dtype))
        args.append(nc.dram_tensor(f"out_{i}_dram", shape, dt, kind="ExternalOutput").ap())
    build(nc, *args)
    r = _run(nc, [arrays], core_ids=[0])
    got = tuple(r.results[0][f"out_{i}_dram"] for i in range(len(_OUTS)))
    return got[0]
```

```python
import concourse.bass as bass
from concourse import mybir
from contextlib import ExitStack

FP32 = mybir.dt.float32
BF16 = mybir.dt.bfloat16
ALU = mybir.AluOpType
ACT = mybir.ActivationFunctionType
AX = mybir.AxisListType

B, T, C = 4, 2048, 256
H = 16
D = C // H
P = 128
CB = C // P
CH = 512
NTILE = B * T // P
TPC = CH // P
CPB = T // CH
TPB = T // P
QH = 4
QPB = H // QH
NQ = B * QPB
PAD = 32
NS = 3
SCALE = 1.0 / float(D) ** 0.5
MA_K, SLOPE, EPS = 0.02, 0.02, 1e-5
MASKED = -1.0e30
Q_PARTS = (0, 1, 2, 0, 1, 0)
K_PARTS = (0, 0, 0, 1, 1, 2)
SR = D * len(Q_PARTS)
MR = SR + NS


START = 16


def at(i, count=1):
    return slice(i, i + count) if isinstance(i, int) else bass.ds(i, count)


class Scratch:

    def __init__(self, nc):
        def dram(name, shape, dt):
            return nc.dram_tensor(name, shape, dt, kind="Internal").ap()
        self.xn = dram("xn_scratch", [B * T + 1, C], FP32)
        self.v = dram("v_scratch", [NQ, T, QH * PAD], FP32)
        self.q = dram("q_scratch", [NQ, NS, QH * D, T], BF16)
        self.k = dram("k_scratch", [NQ, NS, QH * D, T], BF16)
        self.qa = dram("qa_scratch", [B, CB, P, T], FP32)
        self.ka = dram("ka_scratch", [B * T, C], FP32)
        self.res = dram("res_scratch", [B * T, C], FP32)
        self.y = dram("y_scratch", [NQ, P, T], FP32)


def project_stage(nc, ap, scr):
    with ExitStack() as ctx:
        def sb(name, shape, dt=FP32):
            return ctx.enter_context(nc.sbuf_tensor(name, shape, dt))

        def sem(name):
            return ctx.enter_context(nc.semaphore(name))

        x_all = sb("x_all", [P, NTILE, C])
        stats = sb("stats", [P, NTILE, 6])
        mv = sb("mv", [P, NTILE, 2])
        var = sb("var", [P, NTILE])
        std = sb("std", [P, NTILE])
        inv = sb("inv", [P, NTILE])
        t1 = sb("t1", [P, NTILE])
        t2 = sb("t2", [P, NTILE])
        rstd = sb("rstd", [P, NTILE])
        w_attn = sb("w_attn", [P, CB, 2 * C])
        w_k2 = sb("w_k2", [P, CB, C])
        w_ffn = [sb(f"w_ffn{i}", [P, CB, C]) for i in range(3)]
        w_ffn_t = [sb(f"w_ffn_t{i}", [P, CB, C]) for i in range(3)]
        mu = sb("mu", [P, 2, CB])
        eps = sb("eps", [P, 1])
        zrow = sb("zrow", [1, C])
        ident = sb("p_ident", [P, P])
        xn = [sb(f"xn{i}", [P, TPC, C]) for i in range(2)]
        vpad = [sb(f"vpad{i}", [P, TPC, H, PAD]) for i in range(2)]
        xnt = [sb(f"xnt{i}", [P, CB, CH + 1]) for i in range(2)]
        diff = sb("diff", [P, CB, CH])
        xr = sb("xr", [P, CB, CH])
        xk = sb("xk", [P, CB, CH])
        part = sb("part", [P, 4, NS, CH], BF16)
        rest = [sb(f"rest{i}", [P, CH]) for i in range(2)]
        qan = sb("qan", [P, CB, CH])
        ka = sb("ka", [P, TPC, C])
        rgate = sb("rgate", [P, TPC, C])
        krelu = sb("krelu", [P, CB, CH])
        kact = sb("kact", [P, CB, CH])
        res = sb("res", [P, TPC, C])
        bank = [ctx.enter_context(nc.psum_tensor(f"pbank{i}", [P, CH], FP32)) for i in range(8)]

        x_loaded = [sem(f"x_loaded{b}") for b in range(B)]
        w_loaded = sem("w_loaded")
        consts = sem("p_consts")
        zeroed = sem("p_zeroed")
        wt_done = sem("wt_done")
        wt_copied = sem("wt_copied")
        stat_done = sem("stat_done")
        mv_done = sem("mv_done")
        chain = sem("rstd_chain")
        std_done = sem("std_done")
        tail_stored = sem("tail_stored")
        loop_sems = []

        def loop_sem(name):
            loop_sems.append(sem(name))
            return loop_sems[-1]

        xn_done = loop_sem("xn_done")
        vpad_done = loop_sem("vpad_done")
        xt_done = loop_sem("xt_done")
        xnt_copied = loop_sem("xnt_copied")
        edge_done = loop_sem("edge_done")
        diff_done = loop_sem("diff_done")
        mixed = loop_sem("mixed")
        qk_done = loop_sem("qk_done")
        hi_done = loop_sem("hi_done")
        rest_done = loop_sem("rest_done")
        mid_done = loop_sem("mid_done")
        low_done = loop_sem("low_done")
        slope_done = loop_sem("slope_done")
        qan_done = loop_sem("qan_done")
        k2_done = loop_sem("k2_done")
        ka_done = loop_sem("ka_done")
        kt_done = loop_sem("kt_done")
        relu_done = loop_sem("relu_done")
        kact_done = loop_sem("kact_done")
        r_done = loop_sem("r_done")
        gate_done = loop_sem("gate_done")
        v_done = loop_sem("v_done")
        rv_done = loop_sem("rv_done")
        res_done = loop_sem("res_done")
        xn_stored = [loop_sem(f"xn_stored{i}") for i in range(2)]
        v_stored = [loop_sem(f"v_stored{i}") for i in range(2)]
        part_stored = loop_sem("part_stored")
        qan_stored = loop_sem("qan_stored")
        ka_stored = loop_sem("ka_stored")
        res_stored = loop_sem("res_stored")
        gate = sem("p_gate")
        NC = B * CPB

        x_rows = ap["x"].rearrange("b (n p) c -> p (b n) c", p=P)

        with nc.Block() as block:
            @block.sync
            def _(sp):
                for s in loop_sems:
                    sp.sem_inc(s, START)
                for b in range(B):
                    sp.dma_start(x_all[:, TPB * b:TPB * (b + 1), :],
                                 x_rows[:, TPB * b:TPB * (b + 1), :]).then_inc(x_loaded[b], 16)
                sp.wait_ge(zeroed, 1)
                sp.dma_start(scr.xn[B * T:B * T + 1, :], zrow[:, :]).then_inc(tail_stored, 16)
                sp.wait_ge(tail_stored, 16)

            @block.gpsimd
            def _(pool):
                nc.gpsimd.memset(zrow[:, :], 0.0).then_inc(zeroed, 1)
                nc.gpsimd.memset(ident[:, :], 0.0).then_inc(consts, 1)
                nc.gpsimd.memset(eps[:, :], EPS).then_inc(consts, 1)
                for i in range(2):
                    nc.gpsimd.memset(vpad[i][:, :, :, :], 0.0).then_inc(consts, 1)
                pool.wait_ge(consts, 4)
                nc.gpsimd.affine_select(out=ident[:, :], in_=ident[:, :], compare_op=ALU.not_equal, fill=1.0,
                                        base=0, pattern=[[-1, P]], channel_multiplier=1).then_inc(consts, 1)
                for i in range(2):
                    nc.gpsimd.memset(vpad[i][:, :, :, D:D + 1], 1.0).then_inc(consts, 1)

            @block.scalar
            def _(act):
                act.dma_start(w_attn[:, :, :], ap["w_attn"].rearrange("(k p) n -> p k n", p=P)).then_inc(w_loaded, 16)
                act.dma_start(w_k2[:, :, :], ap["w_k2"].rearrange("(k p) n -> p k n", p=P)).then_inc(w_loaded, 16)
                for i, name in enumerate(("w_r", "w_k", "w_v")):
                    act.dma_start(w_ffn[i][:, :, :],
                                  ap[name].rearrange("(k p) n -> p k n", p=P)).then_inc(w_loaded, 16)
                with nc.allow_non_contiguous_dma(reason="256 mixing weights, one per partition"):
                    for i, name in enumerate(("mu_r", "mu_k")):
                        act.dma_start(mu[:, i, :], ap[name].rearrange("(k p) -> p k", p=P)).then_inc(w_loaded, 16)
                for i in range(3):
                    for k in range(CB):
                        act.wait_ge(wt_done, CB * i + k + 1)
                        nc.scalar.activation(w_ffn_t[i][:, k, :], bank[CB * i + k][:, 0:C],
                                             ACT.Copy).then_inc(wt_copied, 1)
                act.wait_ge(mv_done, NTILE)
                act.wait_ge(consts, 5)
                nc.scalar.activation(std[:, :], mv[:, :, 1], ACT.Sqrt, bias=eps[:, :]).then_inc(std_done, 1)
                act.wait_ge(w_loaded, 16 * 7)

            @block.tensor
            def _(pe):
                pe.wait_ge(w_loaded, 16 * 7)
                pe.wait_ge(consts, 5)
                for i in range(3):
                    for k in range(CB):
                        for m in range(CB):
                            last = nc.tensor.transpose(bank[CB * i + k][:, P * m:P * (m + 1)],
                                                       w_ffn[i][:, m, P * k:P * (k + 1)], ident[:, :])
                        last.then_inc(wt_done, 1)

            @block.vector
            def _(dve):
                for b in range(B):
                    dve.wait_ge(x_loaded[b], 16)
                    for n in range(TPB * b, TPB * (b + 1)):
                        nc.vector.bn_stats(stats[:, n, :], x_all[:, n, :]).then_inc(stat_done, 1)
                for n in range(NTILE):
                    dve.wait_ge(stat_done, n + 1)
                    nc.vector.bn_aggr(mv[:, n, :], stats[:, n, :]).then_inc(mv_done, 1)
                dve.wait_ge(mv_done, NTILE)
                nc.vector.tensor_scalar(var[:, :], mv[:, :, 1], EPS, None, ALU.add).then_inc(chain, 1)
                dve.wait_ge(std_done, 1)
                nc.vector.reciprocal(inv[:, :], std[:, :]).then_inc(chain, 1)
                dve.wait_ge(chain, 2)
                nc.vector.tensor_tensor(t1[:, :], inv[:, :], inv[:, :], ALU.mult).then_inc(chain, 1)
                dve.wait_ge(chain, 3)
                nc.vector.tensor_tensor(t2[:, :], t1[:, :], var[:, :], ALU.mult).then_inc(chain, 1)
                dve.wait_ge(chain, 4)
                nc.vector.tensor_scalar(t1[:, :], t2[:, :], -0.5, 1.5, ALU.mult, ALU.add).then_inc(chain, 1)
                dve.wait_ge(chain, 5)
                nc.vector.tensor_tensor(rstd[:, :], t1[:, :], inv[:, :], ALU.mult).then_inc(chain, 1)
                dve.wait_ge(chain, 6)

        with nc.Block() as block:
            @block.vector
            def _(dve):
                def normalise(c, tile0):
                    for j in range(TPC):
                        i = at(tile0 + j)
                        nc.vector.tensor_scalar(xn[c % 2][:, j, :], x_all[:, i, :].rearrange("p a c -> p (a c)"),
                                                mv[:, i, 0:1].rearrange("p a c -> p (a c)"), rstd[:, i],
                                                ALU.subtract, ALU.mult).then_inc(xn_done, 1)

                def batch(b, last):
                    for c in range(CPB):
                        n = b * CPB + c
                        cur, prev = xnt[c % 2], xnt[(c + 1) % 2]
                        dve.wait_ge(xnt_copied, START + n * CB + CB)
                        dve.wait_ge(mixed, START + n * 4)
                        if c == 0:
                            nc.vector.memset(cur[:, :, 0:1], 0.0).then_inc(edge_done, 1)
                        else:
                            nc.vector.tensor_copy(cur[:, :, 0:1], prev[:, :, CH:CH + 1]).then_inc(edge_done, 1)
                        dve.wait_ge(edge_done, START + n + 1)
                        nc.vector.tensor_tensor(diff[:, :, :], cur[:, :, 1:CH + 1], cur[:, :, 0:CH],
                                                ALU.subtract).then_inc(diff_done, 1)
                        dve.wait_ge(diff_done, START + n + 1)
                        for use, dst, free in ((1, xk, kt_done), (0, xr, r_done)):
                            dve.wait_ge(free, START + n * 2)
                            for k in range(CB):
                                nc.vector.scalar_tensor_tensor(
                                    out=dst[:, k, :], in0=diff[:, k, :], scalar=mu[:, use, k:k + 1],
                                    in1=cur[:, k, 0:CH], op0=ALU.mult, op1=ALU.add).then_inc(mixed, 1)
                        for m in range(4):
                            dve.wait_ge(hi_done, START + n * 4 + m + 1)
                            dve.wait_ge(low_done, START + n * 4 + m - 1)
                            if m < CB:
                                dve.wait_ge(slope_done, START + n * 2 + m + 1)
                            nc.vector.tensor_tensor(rest[m % 2][:, :], bank[2 + m][:, :], part[:, m, 0, :],
                                                    ALU.subtract).then_inc(rest_done, 1)
                            if m < CB:
                                nc.vector.scalar_tensor_tensor(out=qan[:, m, :], in0=bank[2 + m][:, :], scalar=-SCALE,
                                                               in1=qan[:, m, :], op0=ALU.mult,
                                                               op1=ALU.max).then_inc(qan_done, 1)
                        if not (last and c == CPB - 1):
                            dve.wait_ge(xt_done, START + n * CB)
                            dve.wait_ge(vpad_done, START + n)
                            dve.wait_ge(xn_stored[(c + 1) % 2], START + (b * 2 + (c + 1) // 2) * 16)
                            normalise(c + 1, n * TPC + TPC)
                        dve.wait_ge(res_stored, START + n * 16)
                        for u in range(2):
                            dve.wait_ge(v_done, START + n * 2 + u + 1)
                            dve.wait_ge(gate_done, START + n * 2 + u + 1)
                            gate = rgate[:, 2 * u:2 * u + 2, :].rearrange("p a c -> p (a c)")
                            out = res[:, 2 * u:2 * u + 2, :].rearrange("p a c -> p (a c)")
                            nc.vector.tensor_tensor(out, bank[4 + u][:, :], gate, ALU.mult).then_inc(rv_done, 1)
                            dve.wait_ge(rv_done, START + n * 2 + u + 1)
                            nc.vector.tensor_tensor(
                                out, out, x_all[:, at(n * TPC + 2 * u, 2), :].rearrange("p a c -> p (a c)"),
                                ALU.add).then_inc(res_done, 1)

                normalise(0, 0)
                with dve.Fori(0, B - 1) as b:
                    batch(b, False)
                batch(B - 1, True)

            @block.tensor
            def _(pe):
                def transpose_chunk(c, n):
                    pe.wait_ge(xn_done, START + n * TPC + TPC)
                    pe.wait_ge(relu_done, START + n * 2)
                    for k in range(CB):
                        for j in range(TPC):
                            last = nc.tensor.transpose(bank[k][:, P * j:P * (j + 1)],
                                                       xn[c % 2][:, j, P * k:P * (k + 1)], ident[:, :])
                        last.then_inc(xt_done, 1)

                def batch(b, last_batch):
                    for c in range(CPB):
                        n = b * CPB + c
                        xt = xnt[c % 2]
                        pe.wait_ge(xnt_copied, START + n * CB + CB)
                        for m in range(4):
                            pe.wait_ge(gate_done if m < 2 else rv_done, START + n * 2)
                            for k in range(CB):
                                last = nc.tensor.matmul(bank[2 + m][:, :], w_attn[:, k, P * m:P * (m + 1)],
                                                        xt[:, k, 1:CH + 1], start=(k == 0), stop=(k == CB - 1))
                            last.then_inc(qk_done, 1)
                        pe.wait_ge(ka_done, START + n * 2)
                        for u in range(2):
                            for j in range(2):
                                t0 = 1 + P * (2 * u + j)
                                for k in range(CB):
                                    last = nc.tensor.matmul(bank[6 + u][:, C * j:C * (j + 1)], xt[:, k, t0:t0 + P],
                                                            w_k2[:, k, :], start=(k == 0), stop=(k == CB - 1))
                            last.then_inc(k2_done, 1)
                        pe.wait_ge(mixed, START + n * 4 + 2)
                        for m in range(CB):
                            for k in range(CB):
                                last = nc.tensor.matmul(bank[m][:, :], w_ffn_t[1][:, k, P * m:P * (m + 1)],
                                                        xk[:, k, :], start=(k == 0), stop=(k == CB - 1))
                            last.then_inc(kt_done, 1)
                        pe.wait_ge(mixed, START + n * 4 + 4)
                        pe.wait_ge(rest_done, START + n * 4 + 2)
                        pe.wait_ge(qan_done, START + n * 2 + 2)
                        for u in range(2):
                            for j in range(2):
                                t0 = P * (2 * u + j)
                                for k in range(CB):
                                    last = nc.tensor.matmul(bank[2 + u][:, C * j:C * (j + 1)], xr[:, k, t0:t0 + P],
                                                            w_ffn_t[0][:, k, :], start=(k == 0), stop=(k == CB - 1))
                            last.then_inc(r_done, 1)
                        if not (last_batch and c == CPB - 1):
                            transpose_chunk(c + 1, n + 1)
                        pe.wait_ge(kact_done, START + n * 2 + 2)
                        pe.wait_ge(rest_done, START + n * 4 + 4)
                        for u in range(2):
                            for j in range(2):
                                t0 = P * (2 * u + j)
                                for k in range(CB):
                                    last = nc.tensor.matmul(bank[4 + u][:, C * j:C * (j + 1)], kact[:, k, t0:t0 + P],
                                                            w_ffn_t[2][:, k, :], start=(k == 0), stop=(k == CB - 1))
                            last.then_inc(v_done, 1)

                transpose_chunk(0, 0)
                with pe.Fori(0, B - 1) as b:
                    batch(b, False)
                batch(B - 1, True)

            @block.scalar
            def _(act):
                def copy_xnt(c, n):
                    act.wait_ge(mixed, START + n * 4 - 4)
                    act.wait_ge(edge_done, START + n)
                    for k in range(CB):
                        act.wait_ge(xt_done, START + n * CB + k + 1)
                        nc.scalar.activation(xnt[c % 2][:, k, 1:CH + 1], bank[k][:, :],
                                             ACT.Copy).then_inc(xnt_copied, 1)

                def batch(b, last):
                    for c in range(CPB):
                        n = b * CPB + c
                        act.wait_ge(part_stored, START + n * 16 * 8)
                        act.wait_ge(qan_stored, START + n * 16)
                        for m in range(4):
                            act.wait_ge(qk_done, START + n * 4 + m + 1)
                            nc.scalar.activation(part[:, m, 0, :], bank[2 + m][:, :], ACT.Copy).then_inc(hi_done, 1)
                            if m < CB:
                                nc.scalar.activation(qan[:, m, :], bank[2 + m][:, :], ACT.Copy,
                                                     scale=-SCALE * SLOPE).then_inc(slope_done, 1)
                        act.wait_ge(ka_stored, START + n * 16)
                        for u in range(2):
                            act.wait_ge(k2_done, START + n * 2 + u + 1)
                            nc.scalar.activation(ka[:, 2 * u:2 * u + 2, :].rearrange("p a c -> p (a c)"),
                                                 bank[6 + u][:, :], ACT.Sigmoid,
                                                 scale=MA_K * SCALE).then_inc(ka_done, 1)
                        act.wait_ge(kact_done, START + n * 2)
                        for m in range(CB):
                            act.wait_ge(kt_done, START + n * 2 + m + 1)
                            nc.scalar.activation(krelu[:, m, :], bank[m][:, :], ACT.Relu).then_inc(relu_done, 1)
                        act.wait_ge(rv_done, START + n * 2)
                        for u in range(2):
                            act.wait_ge(r_done, START + n * 2 + u + 1)
                            nc.scalar.activation(rgate[:, 2 * u:2 * u + 2, :].rearrange("p a c -> p (a c)"),
                                                 bank[2 + u][:, :], ACT.Sigmoid).then_inc(gate_done, 1)
                        if not (last and c == CPB - 1):
                            copy_xnt(c + 1, n + 1)

                copy_xnt(0, 0)
                with act.Fori(0, B - 1) as b:
                    batch(b, False)
                batch(B - 1, True)

            @block.gpsimd
            def _(pool):
                with pool.Fori(0, B) as b:
                    for c in range(CPB):
                        n = b * CPB + c
                        pool.wait_ge(xn_done, START + n * TPC + TPC)
                        pool.wait_ge(v_stored[c % 2], START + (b * 2 + c // 2) * 16 * QPB)
                        pool.sem_inc(gate, 1)
                        nc.gpsimd.tensor_copy(vpad[c % 2][:, :, :, 0:D].rearrange("p j h d -> p (j h) d"),
                                              xn[c % 2][:, :, :].rearrange("p j (h d) -> p (j h) d", d=D)
                                              ).then_inc(vpad_done, 1)
                        pool.wait_ge(part_stored, START + n * 16 * 8)
                        for m in range(4):
                            pool.wait_ge(rest_done, START + n * 4 + m + 1)
                            pool.sem_inc(gate, 1)
                            nc.gpsimd.tensor_copy(part[:, m, 1, :], rest[m % 2][:, :]).then_inc(mid_done, 1)
                            pool.wait_ge(mid_done, START + n * 4 + m + 1)
                            nc.gpsimd.tensor_tensor(part[:, m, 2, :], rest[m % 2][:, :], part[:, m, 1, :],
                                                    ALU.subtract).then_inc(low_done, 1)
                        pool.wait_ge(v_done, START + n * 2)
                        for m in range(CB):
                            pool.wait_ge(relu_done, START + n * 2 + m + 1)
                            nc.gpsimd.tensor_tensor(kact[:, m, :], krelu[:, m, :], krelu[:, m, :],
                                                    ALU.mult).then_inc(kact_done, 1)

            @block.sync
            def _(sp):
                def rows(dram, n):
                    return dram[at(n * CH, CH), :].rearrange("(j p) c -> p j c", p=P)

                with sp.Fori(0, B) as b:
                    for c in range(CPB):
                        n = b * CPB + c
                        ts = slice(CH * c, CH * (c + 1))
                        sp.wait_ge(xn_done, START + n * TPC + TPC)
                        sp.dma_start(rows(scr.xn, n), xn[c % 2][:, :, :]).then_inc(xn_stored[c % 2], 16)
                        sp.wait_ge(vpad_done, START + n + 1)
                        for qd in range(QPB):
                            sp.dma_start(scr.v[at(b * QPB + qd), ts, :].rearrange("a (j p) w -> p (a j) w", p=P),
                                         vpad[c % 2][:, :, QH * qd:QH * (qd + 1), :].rearrange("p j h w -> p j (h w)")
                                         ).then_inc(v_stored[c % 2], 16)
                        sp.wait_ge(qan_done, START + n * 2 + 2)
                        sp.dma_start(scr.qa[at(b), :, :, ts].rearrange("a k p t -> p (a k) t"),
                                     qan[:, :, :]).then_inc(qan_stored, 16)
                        for m in range(4):
                            sp.wait_ge(low_done, START + n * 4 + m + 1)
                            dst = scr.q if m < 2 else scr.k
                            for half in range(2):
                                sp.dma_start(
                                    dst[at(b * QPB + 2 * (m % 2) + half), :, :, ts].rearrange("a s r t -> (a r) s t"),
                                    part[64 * half:64 * half + 64, m, :, :]).then_inc(part_stored, 16)
                        sp.wait_ge(ka_done, START + n * 2 + 2)
                        sp.dma_start(rows(scr.ka, n), ka[:, :, :]).then_inc(ka_stored, 16)
                        sp.wait_ge(res_done, START + n * 2 + 2)
                        sp.dma_start(rows(scr.res, n), res[:, :, :]).then_inc(res_stored, 16)
                for i in range(2):
                    sp.wait_ge(xn_stored[i], START + NC // 2 * 16)
                    sp.wait_ge(v_stored[i], START + NC // 2 * 16 * QPB)
                sp.wait_ge(part_stored, START + NC * 16 * 8)
                sp.wait_ge(qan_stored, START + NC * 16)
                sp.wait_ge(ka_stored, START + NC * 16)
                sp.wait_ge(res_stored, START + NC * 16)


def attention_stage(nc, scr):
    NK = T // P
    BUFS = 3
    SLOTS = 3
    PAIRS = 3
    RQ = 6
    VQ = 2
    SEGS = CPB
    units = [(i, h, seg) for i in range(NK) for h in range(QH) for seg in range(i // TPC + 1)]
    NU = len(units) + 1
    blocks = [(c, j) for c in range(CPB) for j in range(TPC * (c + 1))]
    NB = len(blocks)
    assert BUFS * NU % SLOTS == 0 and BUFS * NB % PAIRS == 0 and (NQ - 1) % BUFS == 0

    def cut(c, j):
        return max(0, P * (j - TPC * c))

    def width(u):
        i, _, seg = u
        return min(CH, P * (i + 1) - CH * seg)

    cost = [sum(CH - cut(*blk) for blk in blocks[:n + 1]) for n in range(NB)]
    ucost = [sum(width(u) for u in units[:n + 1]) for n in range(len(units))]
    LEAD = 0.90
    quota = [sum(uc <= ucost[-1] * co / (LEAD * cost[-1]) for uc in ucost) for co in cost]
    quota = [min(q, len(units)) for q in quota]
    full = quota.index(len(units))
    turn_at = min(full + 2, NB - 1)

    with ExitStack() as ctx:
        def sb(name, shape, dt=FP32):
            return ctx.enter_context(nc.sbuf_tensor(name, shape, dt))

        def sem(name):
            return ctx.enter_context(nc.semaphore(name))

        qst = [sb(f"qst{i}", [P, QH, T], BF16) for i in range(BUFS)]
        kst = [sb(f"kst{i}", [P, QH, T], BF16) for i in range(BUFS)]
        val = [sb(f"val{i}", [P, NK, QH * PAD]) for i in range(BUFS)]
        prob = [sb(f"prob{i}", [P, 2, CH]) for i in range(2 * PAIRS)]
        yt = [sb(f"yt{i}", [P, CH]) for i in range(2)]
        pmax = sb("pmax", [P, NK * QH, SEGS])
        nmax = sb("nmax", [P, NK * QH])
        nrest = sb("nrest", [P, NK * QH])
        npart = sb("npart", [P, NS, NK * QH], BF16)
        mrow = sb("mrow", [NK * QH, NS, P], BF16)
        ident = sb("a_ident", [P, P], BF16)
        mask_kq = sb("mask_kq", [P, P], BF16)
        mask_qk = sb("mask_qk", [P, P], BF16)
        score = [ctx.enter_context(nc.psum_tensor(f"score{i}", [P, 2, CH], FP32)) for i in range(2)]
        acc = ctx.enter_context(nc.psum_tensor("acc", [P, CH], FP32))
        slot = [ctx.enter_context(nc.psum_tensor(f"slot{i}", [P, CH], FP32)) for i in range(SLOTS)]

        consts = sem("a_consts")
        loop_sems = []

        def loop_sem(name):
            loop_sems.append(sem(name))
            return loop_sems[-1]

        q_loaded = [loop_sem(f"q_loaded{i}") for i in range(BUFS)]
        v_loaded = [loop_sem(f"v_loaded{i}") for i in range(BUFS)]
        m_loaded = [loop_sem(f"m_loaded{i}") for i in range(BUFS)]
        peak_scored = loop_sem("peak_scored")
        peak_read = loop_sem("peak_read")
        nmax_done = loop_sem("nmax_done")
        scored = loop_sem("scored")
        exp_done = loop_sem("exp_done")
        pv_done = loop_sem("pv_done")
        acc_copied = loop_sem("acc_copied")
        gate = sem("a_gate")
        y_stored = [loop_sem(f"y_stored{i}") for i in range(2)]

        with nc.Block() as block:
            @block.sync
            def _(sp):
                for s in loop_sems:
                    sp.sem_inc(s, START)

            @block.vector
            def _(dve):
                nc.vector.memset(pmax[:, :, :], -3.0e38).then_inc(consts, 1)
                for i in range(BUFS):
                    nc.vector.memset(kst[i][SR:MR, :, :], 1.0).then_inc(consts, 1)

            @block.gpsimd
            def _(pool):
                nc.gpsimd.memset(ident[:, :], 0.0).then_inc(consts, 1)
                nc.gpsimd.memset(mask_kq[:, :], 0.0).then_inc(consts, 1)
                nc.gpsimd.memset(mask_qk[:, :], 0.0).then_inc(consts, 1)
                pool.wait_ge(consts, BUFS + 4)
                nc.gpsimd.affine_select(out=ident[:, :], in_=ident[:, :], compare_op=ALU.not_equal, fill=1.0,
                                        base=0, pattern=[[-1, P]], channel_multiplier=1).then_inc(consts, 1)
                nc.gpsimd.affine_select(out=mask_kq[:, :], in_=mask_kq[:, :], compare_op=ALU.is_ge, fill=MASKED,
                                        base=0, pattern=[[1, P]], channel_multiplier=-1).then_inc(consts, 1)
                nc.gpsimd.affine_select(out=mask_qk[:, :], in_=mask_qk[:, :], compare_op=ALU.is_ge, fill=MASKED,
                                        base=0, pattern=[[-1, P]], channel_multiplier=1).then_inc(consts, 1)

        def steps(eng, step):
            step(0, 0, True, False)
            with eng.Fori(0, (NQ - 1) // BUFS) as r:
                for s in range(1, BUFS + 1):
                    step(r, s, True, True)
            step(NQ // BUFS, NQ % BUFS, False, True)

        def filled(r, s):
            return r + s // BUFS + 1

        with nc.Block() as block:
            @block.sync
            def _(sp):
                def load(n, buf):
                    for i, part in enumerate(Q_PARTS):
                        sp.dma_start(qst[buf][D * i:D * (i + 1), :, :],
                                     scr.q[at(n), part, :, :].rearrange("a (h d) t -> d (a h) t", d=D)
                                     ).then_inc(q_loaded[buf], 16)
                    for i, part in enumerate(K_PARTS):
                        sp.dma_start(kst[buf][D * i:D * (i + 1), :, :],
                                     scr.k[at(n), part, :, :].rearrange("a (h d) t -> d (a h) t", d=D)
                                     ).then_inc(q_loaded[buf], 16)
                    for i in range(VQ):
                        some = slice(NK // VQ * i, NK // VQ * (i + 1))
                        sp.dma_start(val[buf][:, some, :],
                                     scr.v[at(n), :, :].rearrange("a (j p) w -> p (a j) w", p=P)[:, some, :]
                                     ).then_inc(v_loaded[buf], 16)

                def store(n, c):
                    sp.wait_ge(acc_copied, START + (n - 1) * CPB + c + 1)
                    sp.dma_start(scr.y[at(n - 1), :, CH * c:CH * (c + 1)].rearrange("a p t -> (a p) t"),
                                 yt[c % 2][:, :]).then_inc(y_stored[c % 2], 16)

                def rows(n, buf):
                    sp.wait_ge(peak_read, START + n * NU + NU)
                    for i in range(NS):
                        sp.dma_start(qst[buf][SR + i:SR + i + 1, :, :].rearrange("a h (i t) -> a (h i) t", t=P),
                                     mrow[:, i, :]).then_inc(m_loaded[buf], 16)

                def step(r, s, more):
                    n = r * BUFS + s
                    sp.wait_ge(pv_done, START + (n - 1) * NB)
                    if more:
                        load(n + 1, (s + 1) % BUFS)
                    for c in range(CPB - 1):
                        store(n, c)
                    rows(n, s % BUFS)
                    store(n, CPB - 1)

                load(0, 0)
                load(1, 1)
                rows(0, 0)
                with sp.Fori(0, (NQ - 1) // BUFS - 1) as r:
                    for s in range(1, BUFS + 1):
                        step(r, s, True)
                for s in range(1, BUFS + 1):
                    step((NQ - 1) // BUFS - 1, s, s < BUFS)
                for c in range(CPB):
                    store(NQ, c)
                for i in range(2):
                    sp.wait_ge(y_stored[i], START + NQ * CPB // 2 * 16)

            @block.tensor
            def _(pe):
                def peak(r, s, w):
                    n = r * BUFS + s
                    buf, dst = s % BUFS, slot[(NU * s + w) % SLOTS]
                    i, h, seg = units[w]
                    wd = width(units[w])
                    diag = seg == i // TPC
                    pe.wait_ge(peak_read, START + n * NU + w - SLOTS + 1)
                    last = nc.tensor.matmul(dst[:, 0:wd], qst[buf][0:SR, h, P * i:P * (i + 1)],
                                            kst[buf][0:SR, h, CH * seg:CH * seg + wd], start=True, stop=not diag)
                    if diag:
                        last = nc.tensor.matmul(dst[:, wd - P:wd], ident[:, :], mask_qk[:, :], start=False, stop=True)
                    last.then_inc(peak_scored, 1)

                def turn(r, s):
                    n = r * BUFS + s
                    dst = slot[(NU * s + NU - 1) % SLOTS][:, :].bitcast(BF16)
                    pe.wait_ge(peak_read, START + n * NU + NU - SLOTS)
                    pe.wait_ge(nmax_done, START + n * 5 + 5)
                    pe.sem_inc(gate, 1)
                    for i in range(NS):
                        last = nc.tensor.transpose(dst[0:NK * QH, P * i:P * (i + 1)], npart[:, i, :], ident[:, :])
                    last.then_inc(peak_scored, 1)

                def scores(r, s, b, half):
                    m = r * BUFS + s - 1
                    c, j = blocks[b]
                    q, k, dst = qst[(s - 1) % BUFS], kst[(s - 1) % BUFS], score[half]
                    t0 = CH * c + cut(c, j)
                    wd = CH - cut(c, j)
                    diag = j >= TPC * c
                    pe.wait_ge(exp_done, START + m * 2 * NB + 2 * b + half - 1)
                    for e in range(2):
                        h = 2 * half + e
                        last = nc.tensor.matmul(dst[:, e, 0:wd], k[0:MR, h, P * j:P * (j + 1)],
                                                q[0:MR, h, t0:t0 + wd], start=True, stop=not diag)
                        if diag:
                            last = nc.tensor.matmul(dst[:, e, 0:P], ident[:, :], mask_kq[:, :],
                                                    start=False, stop=True)
                    last.then_inc(scored, 1)

                def product(r, s, b):
                    m = r * BUFS + s - 1
                    c, j = blocks[b]
                    v = val[(s - 1) % BUFS]
                    wd = CH - cut(c, j)
                    pe.wait_ge(exp_done, START + m * 2 * NB + 2 * b + 2)
                    if j == 0:
                        pe.wait_ge(acc_copied, START + m * CPB + c)
                    for h in range(QH):
                        p = prob[(2 * (NB * (s - 1) + b) + h // 2) % (2 * PAIRS)]
                        last = nc.tensor.matmul(acc[PAD * h:PAD * (h + 1), cut(c, j):CH],
                                                v[:, j, PAD * h:PAD * (h + 1)], p[:, h % 2, 0:wd],
                                                start=(j == 0), stop=(j == TPC * (c + 1) - 1))
                    last.then_inc(pv_done, 1)

                def step(r, s, peaks, main):
                    if peaks:
                        pe.wait_ge(q_loaded[s % BUFS], START + 16 * 2 * RQ * filled(r, s))
                    if not main:
                        for w in range(len(units)):
                            peak(r, s, w)
                        turn(r, s)
                        return
                    pe.wait_ge(m_loaded[(s - 1) % BUFS], START + 16 * NS * filled(r, s - 1))
                    pe.wait_ge(v_loaded[(s - 1) % BUFS], START + 16 * VQ * filled(r, s - 1))
                    done = 0
                    for b in range(NB):
                        todo = quota[b] - done if peaks else 0
                        gap = [todo // 3 + (todo % 3 > x) for x in range(3)]
                        for x in range(3):
                            if x < 2:
                                scores(r, s, b, x)
                            elif b > 0:
                                product(r, s, b - 1)
                            for _ in range(gap[x]):
                                peak(r, s, done)
                                done += 1
                        if peaks and b == turn_at:
                            turn(r, s)
                    product(r, s, NB - 1)

                pe.wait_ge(consts, BUFS + 7)
                steps(pe, step)

            @block.scalar
            def _(act):
                def step(r, s, peaks, main):
                    if not main:
                        return
                    m = r * BUFS + s - 1
                    for b, (c, j) in enumerate(blocks):
                        wd = CH - cut(c, j)
                        act.wait_ge(pv_done, START + m * NB + b - PAIRS + 1)
                        for half in range(2):
                            p = prob[(2 * (NB * (s - 1) + b) + half) % (2 * PAIRS)]
                            act.wait_ge(scored, START + m * 2 * NB + 2 * b + half + 1)
                            nc.scalar.activation(p[:, :, 0:wd], score[half][:, :, 0:wd], ACT.Exp,
                                                 scale=SCALE).then_inc(exp_done, 1)
                        if c and j == 0:
                            copy_sums(m, c - 1, b)
                    copy_sums(m, CPB - 1, NB)

                def copy_sums(m, c, products):
                    act.wait_ge(pv_done, START + m * NB + products)
                    act.wait_ge(y_stored[c % 2], START + (m * (CPB // 2) + c // 2) * 16)
                    nc.scalar.activation(yt[c % 2][:, :], acc[:, :], ACT.Copy).then_inc(acc_copied, 1)

                steps(act, step)

            @block.vector
            def _(dve):
                def step(r, s, peaks, main):
                    if not peaks:
                        return
                    n = r * BUFS + s
                    for w, u in enumerate(units):
                        i, h, seg = u
                        dve.wait_ge(peak_scored, START + n * NU + w + 1)
                        if w == 0:
                            dve.wait_ge(nmax_done, START + n * 5)
                        nc.vector.tensor_reduce(pmax[:, NK * h + i, seg:seg + 1],
                                                slot[(NU * s + w) % SLOTS][:, 0:width(u)], AX.X,
                                                ALU.max).then_inc(peak_read, 1)
                    dve.wait_ge(peak_read, START + n * NU + NU - 1)
                    nc.vector.tensor_reduce(nmax[:, :], pmax[:, :, :], AX.X, ALU.max, negate=True
                                            ).then_inc(nmax_done, 1)
                    dve.wait_ge(nmax_done, START + n * 5 + 1)
                    nc.vector.tensor_copy(npart[:, 0, :], nmax[:, :]).then_inc(nmax_done, 1)
                    dve.wait_ge(nmax_done, START + n * 5 + 2)
                    nc.vector.tensor_tensor(nrest[:, :], nmax[:, :], npart[:, 0, :], ALU.subtract
                                            ).then_inc(nmax_done, 1)
                    dve.wait_ge(nmax_done, START + n * 5 + 3)
                    nc.vector.tensor_copy(npart[:, 1, :], nrest[:, :]).then_inc(nmax_done, 1)
                    dve.wait_ge(nmax_done, START + n * 5 + 4)
                    nc.vector.tensor_tensor(npart[:, 2, :], nrest[:, :], npart[:, 1, :], ALU.subtract
                                            ).then_inc(nmax_done, 1)
                    dve.wait_ge(peak_scored, START + n * NU + NU)
                    back = (s - 1) % BUFS
                    fills = r + (s - 1) // BUFS + 1
                    dve.wait_ge(m_loaded[back], START + 16 * NS * fills)
                    nc.vector.tensor_copy(mrow[:, :, :].rearrange("p s t -> p (s t)"),
                                          slot[(NU * s + NU - 1) % SLOTS][:, :].bitcast(BF16)[0:NK * QH, 0:NS * P]
                                          ).then_inc(peak_read, 1)

                dve.wait_ge(consts, BUFS + 7)
                steps(dve, step)


def mix_stage(nc, ap, scr):
    TILES = 2
    NI = TILES * B
    STEPS = TPB // TILES
    GH = P // D
    LOADS = 5 + GH
    with ExitStack() as ctx:
        def sb(name, shape, dt=FP32):
            return ctx.enter_context(nc.sbuf_tensor(name, shape, dt))

        def sem(name):
            return ctx.enter_context(nc.semaphore(name))

        w_proj = sb("w_proj", [P, CB, C])
        ident = sb("m_ident", [P, P])
        strict = sb("strict", [P, P])
        own = sb("own", [P, H])
        yraw = [sb(f"yraw{i}", [P, QPB, TILES * P]) for i in range(B)]
        vnext = [sb(f"vnext{i}", [P, TILES, C]) for i in range(B)]
        qa = [sb(f"qa{i}", [P, CB, TILES * P]) for i in range(B)]
        qexp = [sb(f"qexp{i}", [P, CB, GH, TILES * P]) for i in range(B)]
        ka = [sb(f"ka{i}", [P, TILES, C]) for i in range(B)]
        res = [sb(f"mres{i}", [P, TILES, C]) for i in range(B)]
        state = [sb(f"state{i}", [P, C]) for i in range(B)]
        kat = [sb(f"kat{i}", [P, CB, P]) for i in range(2)]
        den = [sb(f"den{i}", [P, H]) for i in range(2)]
        y = [sb(f"y{i}", [P, H, D]) for i in range(2)]
        e = [sb(f"e{i}", [P, H, PAD]) for i in range(2)]
        am = [sb(f"am{i}", [P, QPB, QH, P]) for i in range(2)]
        snew = [sb(f"snew{i}", [P, C]) for i in range(2)]
        y2t = [sb(f"y2t{i}", [P, QPB * P]) for i in range(2)]
        yi = [sb(f"yi{i}", [P, H, D]) for i in range(2)]
        ysum = [sb(f"ysum{i}", [P, H, D]) for i in range(2)]
        ysumt = [sb(f"ysumt{i}", [P, CB, P]) for i in range(2)]
        outt = [sb(f"outt{i}", [P, C]) for i in range(2)]
        abank = [ctx.enter_context(nc.psum_tensor(f"abank{i}", [P, QH, P], FP32)) for i in range(QPB)]
        ybank = ctx.enter_context(nc.psum_tensor("ybank", [P, CH], FP32))
        zbank = ctx.enter_context(nc.psum_tensor("zbank", [P, CH], FP32))
        obank = ctx.enter_context(nc.psum_tensor("obank", [P, QPB, P], FP32))
        kbank = ctx.enter_context(nc.psum_tensor("kbank", [P, CH], FP32))

        consts = sem("m_consts")
        zeroed = [sem(f"m_zeroed{i}") for i in range(B)]
        w_loaded = sem("m_w_loaded")
        loop_sems = []

        def loop_sem(name):
            loop_sems.append(sem(name))
            return loop_sems[-1]

        loaded = [loop_sem(f"m_loaded{i}") for i in range(B)]
        yt_done = loop_sem("m_yt")
        den_done = loop_sem("m_den")
        y_done = loop_sem("m_y")
        e_done = loop_sem("m_e")
        kt_done = loop_sem("m_kt")
        kat_done = loop_sem("m_kat")
        a_done = loop_sem("m_a")
        am_done = loop_sem("m_am")
        i_done = loop_sem("m_i")
        yi_done = loop_sem("m_yi")
        o_done = loop_sem("m_o")
        y2t_done = loop_sem("m_y2t")
        s_done = loop_sem("m_s")
        snew_done = loop_sem("m_snew")
        state_done = loop_sem("m_state")
        z_done = loop_sem("m_z")
        ysum_done = loop_sem("m_ysum")
        w_done = loop_sem("m_w")
        ysumt_done = loop_sem("m_ysumt")
        p_done = loop_sem("m_p")
        out_done = loop_sem("m_out")
        stored = [loop_sem(f"m_stored{i}") for i in range(2)]
        CONSTS = 5 + 4 + B

        with nc.Block() as block:
            @block.sync
            def _(sp):
                def load(r, b):
                    col = slice(r * TILES * P, (r + 1) * TILES * P) if isinstance(r, int) \
                        else bass.ds(r * (TILES * P), TILES * P)
                    row = r * (TILES * P) + b * T

                    def tokens(dram, first):
                        return dram[at(first, TILES * P), :].rearrange("(i p) c -> p i c", p=P)

                    sp.dma_start(yraw[b][:, :, :], scr.y[QPB * b:QPB * (b + 1), :, col].rearrange("q p t -> p q t")
                                 ).then_inc(loaded[b], 16)
                    sp.dma_start(ka[b][:, :, :], tokens(scr.ka, row)).then_inc(loaded[b], 16)
                    sp.dma_start(vnext[b][:, :, :], tokens(scr.xn, row + 1)).then_inc(loaded[b], 16)
                    sp.dma_start(qa[b][:, :, :], scr.qa[b, :, :, col].rearrange("k p t -> p k t")
                                 ).then_inc(loaded[b], 16)
                    for h in range(GH):
                        rows = slice(D * h, D * (h + 1))
                        sp.dma_start(qexp[b][rows, :, h, :], scr.qa[b, :, rows, col].rearrange("k p t -> p k t")
                                     ).then_inc(loaded[b], 16)
                    sp.dma_start(res[b][:, :, :], tokens(scr.res, row)).then_inc(loaded[b], 16)

                def store(r, k):
                    m = r * NI + k
                    row = (r * TILES + k // B) * P
                    sp.wait_ge(out_done, START + m + 1)
                    sp.dma_start(ap["out"][k % B, at(row, P), :], outt[k % 2][:, :]).then_inc(stored[k % 2], 16)

                for s in loop_sems:
                    sp.sem_inc(s, START)
                sp.dma_start(w_proj[:, :, :], ap["w_proj"].rearrange("(k p) n -> p k n", p=P)).then_inc(w_loaded, 16)
                for b in range(B):
                    sp.wait_ge(zeroed[b], 1)
                    load(0, b)
                with sp.Fori(0, STEPS - 1) as r:
                    for k in range(NI):
                        store(r, k)
                        if k >= NI - B:
                            load(r + 1, k % B)
                for k in range(NI):
                    store(STEPS - 1, k)
                for i in range(2):
                    sp.wait_ge(stored[i], START + STEPS * NI // 2 * 16)

            @block.tensor
            def _(pe):
                def span(k):
                    return slice(P * (k // B), P * (k // B + 1))

                def turn(r, k):
                    m = r * NI + k
                    b = k % B
                    pe.wait_ge(loaded[b], START + r * (16 * LOADS) + 16 * LOADS)
                    pe.wait_ge(yi_done, START + m)
                    pe.wait_ge(snew_done, START + m - 1)
                    for g in range(CB):
                        last = nc.tensor.transpose(kbank[:, P * g:P * (g + 1)], ka[b][:, k // B, P * g:P * (g + 1)],
                                                   ident[:, :])
                    last.then_inc(kt_done, 1)
                    pe.wait_ge(out_done, START + m - 2)
                    for q in range(QPB):
                        last = nc.tensor.transpose(ybank[:, P * q:P * (q + 1)], yraw[b][:, q, span(k)], ident[:, :])
                    last.then_inc(yt_done, 1)

                def inner(r, k):
                    m = r * NI + k
                    pe.wait_ge(kat_done, START + m + 1)
                    for a in range(QPB):
                        pe.wait_ge(am_done, START + m * QPB - QPB + a + 1)
                        g, h0 = a * QH // GH, a * QH % GH
                        nc.tensor.matmul(abank[a][:, :, :], kat[k % 2][:, g, :],
                                         qexp[k % B][:, g, h0:h0 + QH, span(k)],
                                         start=True, stop=True).then_inc(a_done, 1)

                def carried(r, k):
                    m = r * NI + k
                    pe.wait_ge(state_done, START + m - B + 1)
                    pe.wait_ge(kat_done, START + m + 1)
                    pe.wait_ge(snew_done, START + m)
                    for g in range(CB):
                        last = nc.tensor.matmul(kbank[:, P * g:P * (g + 1)], qa[k % B][:, g, span(k)],
                                                state[k % B][:, P * g:P * (g + 1)], start=True, stop=True)
                    last.then_inc(i_done, 1)

                def apply(r, k):
                    m = r * NI + k
                    pe.wait_ge(y2t_done, START + m)
                    pe.wait_ge(e_done, START + m + 1)
                    pe.wait_ge(am_done, START + m * QPB + QPB)
                    for a in range(QPB):
                        for j in range(QH):
                            last = nc.tensor.matmul(obank[PAD * j:PAD * (j + 1), a, :], e[k % 2][:, QH * a + j, :],
                                                    am[k % 2][:, a, j, :], start=True, stop=True)
                    last.then_inc(o_done, 1)

                def turn_back(r, k):
                    m = r * NI + k
                    pe.wait_ge(y2t_done, START + m + 1)
                    pe.wait_ge(ysumt_done, START + m)
                    for q in range(QPB):
                        last = nc.tensor.transpose(zbank[:, P * q:P * (q + 1)], y2t[k % 2][:, P * q:P * (q + 1)],
                                                   ident[:, :])
                    last.then_inc(z_done, 1)

                def update(r, k, more):
                    m = r * NI + k
                    pe.wait_ge(yi_done, START + m + 1)
                    pe.wait_ge(kat_done, START + m + 1 + more)
                    for g in range(CB):
                        last = nc.tensor.matmul(kbank[:, C + P * g:C + P * (g + 1)],
                                                ka[k % B][:, k // B, P * g:P * (g + 1)],
                                                e[k % 2][:, GH * g:GH * (g + 1), 0:D], start=True, stop=True)
                    last.then_inc(s_done, 1)

                def turn_sum(r, k):
                    m = r * NI + k
                    pe.wait_ge(ysum_done, START + m + 1)
                    for g in range(CB):
                        last = nc.tensor.transpose(
                            zbank[:, P * g:P * (g + 1)],
                            ysum[k % 2][:, GH * g:GH * (g + 1), :].rearrange("p h d -> p (h d)"), ident[:, :])
                    last.then_inc(w_done, 1)

                def project(r, k, ahead):
                    m = r * NI + k
                    pe.wait_ge(ysumt_done, START + m + 1)
                    pe.wait_ge(y_done, START + m + 1 + ahead)
                    pe.wait_ge(out_done, START + m)
                    for g in range(CB):
                        last = nc.tensor.matmul(ybank[:, 0:C], ysumt[k % 2][:, g, :], w_proj[:, g, :],
                                                start=(g == 0), stop=(g == CB - 1))
                    last.then_inc(p_done, 1)

                def step(r, first, last):
                    for k in range(NI):
                        after = not (last and k == NI - 1)
                        before = not (first and k == 0)
                        r1, k1 = r + (k + 1) // NI, (k + 1) % NI
                        r0, k0 = r + (k - 1) // NI, (k - 1) % NI
                        carried(r, k)
                        apply(r, k)
                        if after:
                            turn(r1, k1)
                        if before:
                            turn_sum(r0, k0)
                        if after:
                            inner(r1, k1)
                        turn_back(r, k)
                        update(r, k, after)
                        if before:
                            project(r0, k0, 1 + after)

                pe.wait_ge(consts, CONSTS)
                pe.wait_ge(w_loaded, 16)
                turn(0, 0)
                inner(0, 0)
                step(0, True, False)
                with pe.Fori(1, STEPS - 1) as r:
                    step(r, False, False)
                step(STEPS - 1, False, True)
                turn_sum(STEPS - 1, NI - 1)
                project(STEPS - 1, NI - 1, 0)

            @block.gpsimd
            def _(pool):
                nc.gpsimd.memset(ident[:, :], 0.0).then_inc(consts, 1)
                nc.gpsimd.memset(strict[:, :], 1.0).then_inc(consts, 1)
                nc.gpsimd.memset(own[:, :], 1.0).then_inc(consts, 1)
                for i in range(2):
                    nc.gpsimd.memset(e[i][:, :, :], 0.0).then_inc(consts, 1)
                pool.wait_ge(consts, 5)
                nc.gpsimd.affine_select(out=ident[:, :], in_=ident[:, :], compare_op=ALU.not_equal, fill=1.0,
                                        base=0, pattern=[[-1, P]], channel_multiplier=1).then_inc(consts, 1)
                nc.gpsimd.affine_select(out=strict[:, :], in_=strict[:, :], compare_op=ALU.is_gt, fill=0.0,
                                        base=0, pattern=[[1, P]], channel_multiplier=-1).then_inc(consts, 1)
                rows = own[:, :].rearrange("p (g h) -> p g h", g=CB)
                nc.gpsimd.affine_select(out=rows, in_=rows, compare_op=ALU.is_ge, fill=0.0,
                                        base=0, pattern=[[0, CB], [-D, GH]], channel_multiplier=1).then_inc(consts, 1)
                pool.wait_ge(consts, 8)
                nc.gpsimd.affine_select(out=rows, in_=rows, compare_op=ALU.is_ge, fill=0.0,
                                        base=D - 1, pattern=[[0, CB], [D, GH]],
                                        channel_multiplier=-1).then_inc(consts, 1)
                for b in range(B):
                    nc.gpsimd.memset(state[b][:, :], 0.0).then_inc(consts, 1)
                for b in (2, 3):
                    nc.gpsimd.memset(qexp[b][:, :, :, :], 0.0).then_inc(zeroed[b], 1)

                def error(r, k):
                    m = r * NI + k
                    pool.wait_ge(loaded[k % B], START + r * (16 * LOADS) + 16 * LOADS)
                    pool.wait_ge(y_done, START + m + 1)
                    pool.wait_ge(s_done, START + m - 1)
                    nc.gpsimd.tensor_tensor(e[k % 2][:, :, 0:D], y[k % 2][:, :, :],
                                            vnext[k % B][:, k // B, :].rearrange("p (h d) -> p h d", d=D),
                                            ALU.subtract).then_inc(e_done, 1)

                def keep(r, k):
                    m = r * NI + k
                    pool.wait_ge(i_done, START + m + 1)
                    pool.wait_ge(snew_done, START + m + 1)
                    nc.gpsimd.tensor_tensor(state[k % B][:, :], state[k % B][:, :], snew[k % 2][:, :],
                                            ALU.add).then_inc(state_done, 1)

                pool.wait_ge(consts, CONSTS)
                error(0, 0)
                with pool.Fori(0, STEPS - 1) as r:
                    for k in range(NI):
                        error(r + (k + 1) // NI, (k + 1) % NI)
                        keep(r, k)
                for k in range(NI):
                    if k < NI - 1:
                        error(STEPS - 1, k + 1)
                    keep(STEPS - 1, k)

            @block.scalar
            def _(act):
                def turned(r, k):
                    m = r * NI + k
                    act.wait_ge(kt_done, START + m + 1)
                    act.wait_ge(a_done, START + m * QPB - QPB)
                    nc.scalar.activation(kat[k % 2][:, :, :].rearrange("p g t -> p (g t)"), kbank[:, 0:C],
                                         ACT.Copy).then_inc(kat_done, 1)

                def back(r, k):
                    m = r * NI + k
                    act.wait_ge(o_done, START + m + 1)
                    act.wait_ge(z_done, START + m - 1)
                    nc.scalar.activation(y2t[k % 2][:, :], obank[:, :, :].rearrange("p q t -> p (q t)"),
                                         ACT.Copy).then_inc(y2t_done, 1)

                def both(r, k):
                    m = r * NI + k
                    act.wait_ge(w_done, START + m + 1)
                    act.wait_ge(p_done, START + m - 1)
                    nc.scalar.activation(ysumt[k % 2][:, :, :].rearrange("p g t -> p (g t)"), zbank[:, 0:C],
                                         ACT.Copy).then_inc(ysumt_done, 1)

                def step(r, first, last):
                    for k in range(NI):
                        if not (last and k == NI - 1):
                            turned(r + (k + 1) // NI, (k + 1) % NI)
                        if not (first and k == 0):
                            both(r + (k - 1) // NI, (k - 1) % NI)
                        back(r, k)

                turned(0, 0)
                step(0, True, False)
                with act.Fori(1, STEPS - 1) as r:
                    step(r, False, False)
                step(STEPS - 1, False, True)
                both(STEPS - 1, NI - 1)

            @block.vector
            def _(dve):
                def attention(r, k):
                    m = r * NI + k
                    dve.wait_ge(yt_done, START + m + 1)
                    sums = ybank[:, :].rearrange("p (h w) -> p h w", w=PAD)
                    nc.vector.reciprocal(den[k % 2][:, :], sums[:, :, D]).then_inc(den_done, 1)
                    dve.wait_ge(den_done, START + m + 1)
                    dve.wait_ge(yi_done, START + m - 1)
                    dve.wait_ge(e_done, START + m - 1)
                    nc.vector.tensor_tensor(y[k % 2][:, :, :], sums[:, :, 0:D],
                                            den[k % 2][:, :].unsqueeze(2).to_broadcast([P, H, D]),
                                            ALU.mult).then_inc(y_done, 1)

                def masks(r, k):
                    m = r * NI + k
                    dve.wait_ge(o_done, START + m - 1)
                    for a in range(QPB):
                        dve.wait_ge(a_done, START + m * QPB + a + 1)
                        nc.vector.tensor_tensor(am[k % 2][:, a, :, :], abank[a][:, :, :],
                                                strict[:, :].unsqueeze(1).to_broadcast([P, QH, P]),
                                                ALU.mult).then_inc(am_done, 1)

                def carried(r, k):
                    m = r * NI + k
                    dve.wait_ge(i_done, START + m + 1)
                    dve.wait_ge(y_done, START + m + 1)
                    dve.wait_ge(ysum_done, START + m - 1)
                    nc.vector.tensor_tensor(yi[k % 2][:, :, :], kbank[:, 0:C].rearrange("p (h d) -> p h d", d=D),
                                            y[k % 2][:, :, :], ALU.add).then_inc(yi_done, 1)

                def total(r, k):
                    m = r * NI + k
                    dve.wait_ge(z_done, START + m + 1)
                    dve.wait_ge(yi_done, START + m + 1)
                    dve.wait_ge(w_done, START + m - 1)
                    nc.vector.tensor_tensor(ysum[k % 2][:, :, :],
                                            zbank[:, :].rearrange("p (h w) -> p h w", w=PAD)[:, :, 0:D],
                                            yi[k % 2][:, :, :], ALU.add).then_inc(ysum_done, 1)

                def own_blocks(r, k):
                    m = r * NI + k
                    dve.wait_ge(s_done, START + m + 1)
                    dve.wait_ge(state_done, START + m - 1)
                    nc.vector.tensor_tensor(snew[k % 2][:, :].rearrange("p (h d) -> p h d", d=D),
                                            kbank[:, C:2 * C].rearrange("p (h d) -> p h d", d=D),
                                            own[:, :].unsqueeze(2).to_broadcast([P, H, D]),
                                            ALU.mult).then_inc(snew_done, 1)

                def finish(r, k):
                    m = r * NI + k
                    dve.wait_ge(p_done, START + m + 1)
                    dve.wait_ge(stored[k % 2], START + (r * (NI // 2) + k // 2) * 16)
                    nc.vector.tensor_tensor(outt[k % 2][:, :], ybank[:, 0:C], res[k % B][:, k // B, :],
                                            ALU.add).then_inc(out_done, 1)

                def step(r, first, last):
                    for k in range(NI):
                        r1, k1 = r + (k + 1) // NI, (k + 1) % NI
                        carried(r, k)
                        if not (last and k == NI - 1):
                            attention(r1, k1)
                            masks(r1, k1)
                        own_blocks(r, k)
                        total(r, k)
                        if not (first and k == 0):
                            finish(r + (k - 1) // NI, (k - 1) % NI)

                for b in (0, 1):
                    nc.vector.memset(qexp[b][:, :, :, :], 0.0).then_inc(zeroed[b], 1)
                dve.wait_ge(consts, CONSTS)
                attention(0, 0)
                masks(0, 0)
                step(0, True, False)
                with dve.Fori(1, STEPS - 1) as r:
                    step(r, False, False)
                step(STEPS - 1, False, True)
                finish(STEPS - 1, NI - 1)


def build(nc, x, w_attn, w_k2, w_proj, w_r, w_k, w_v, mu_r, mu_k, out):
    ap = dict(x=x, w_attn=w_attn, w_k2=w_k2, w_proj=w_proj, w_r=w_r, w_k=w_k, w_v=w_v,
              mu_r=mu_r, mu_k=mu_k, out=out)
    scr = Scratch(nc)
    project_stage(nc, ap, scr)
    attention_stage(nc, scr)
    mix_stage(nc, ap, scr)


_INS = ['L0_attn_x', 'L0_attn_W_attn', 'L0_attn_W_k2', 'L0_attn_W_proj', 'L0_ffn_W_r', 'L0_ffn_W_k',
        'L0_ffn_W_v', 'L0_ffn_mu_r', 'L0_ffn_mu_k']
_OUTS = [((B, T, C), 'float32')]


def kernel(**inputs):
    import numpy as _np
    import concourse.bacc as _bacc
    from concourse import mybir as _mybir
    from concourse.bass_utils import run_bass_kernel_spmd as _run

    nc = _bacc.Bacc("TRN2", target_bir_lowering=False, num_devices=1)
    arrays, args = {}, []
    for name in _INS:
        a = _np.ascontiguousarray(inputs[name])
        arrays[f"in_{name}_dram"] = a
        args.append(nc.dram_tensor(f"in_{name}_dram", a.shape, _mybir.dt.from_np(a.dtype), kind="ExternalInput").ap())
    for i, (shape, dtype) in enumerate(_OUTS):
        dt = _mybir.dt.from_np(_np.dtype(dtype))
        args.append(nc.dram_tensor(f"out_{i}_dram", shape, dt, kind="ExternalOutput").ap())
    build(nc, *args)
    r = _run(nc, [arrays], core_ids=[0])
    got = tuple(r.results[0][f"out_{i}_dram"] for i in range(len(_OUTS)))
    return got[0]
```

```python
import concourse.bass as bass
from concourse import mybir
from contextlib import ExitStack

FP32 = mybir.dt.float32
BF16 = mybir.dt.bfloat16
ALU = mybir.AluOpType
ACT = mybir.ActivationFunctionType
AX = mybir.AxisListType

B, T, C = 4, 2048, 256
H = 16
D = C // H
P = 128
CB = C // P
CH = 512
NTILE = B * T // P
TPC = CH // P
CPB = T // CH
TPB = T // P
QH = 4
QPB = H // QH
NQ = B * QPB
PAD = 32
NS = 3
SCALE = 1.0 / float(D) ** 0.5
MA_K, SLOPE, EPS = 0.02, 0.02, 1e-5
MASKED = -1.0e30
Q_PARTS = (0, 1, 2, 0, 1, 0)
K_PARTS = (0, 0, 0, 1, 1, 2)
SR = D * len(Q_PARTS)
MR = SR + NS


START = 16


def at(i, count=1):
    return slice(i, i + count) if isinstance(i, int) else bass.ds(i, count)


class Scratch:

    def __init__(self, nc):
        def dram(name, shape, dt):
            return nc.dram_tensor(name, shape, dt, kind="Internal").ap()
        self.xn = dram("xn_scratch", [B * T + 1, C], FP32)
        self.v = dram("v_scratch", [NQ, T, QH * PAD], FP32)
        self.q = dram("q_scratch", [NQ, NS, QH * D, T], BF16)
        self.k = dram("k_scratch", [NQ, NS, QH * D, T], BF16)
        self.qa_part = dram("qa_part_scratch", [B, NS, C, T], BF16)
        self.ka_part = dram("ka_part_scratch", [B, NS, C, T], BF16)
        self.qa = dram("qa_scratch", [B, CB, P, T], FP32)
        self.ka = dram("ka_scratch", [B * T, C], FP32)
        self.res = dram("res_scratch", [B * T, C], FP32)
        self.y = dram("y_scratch", [NQ, P, T], FP32)


def project_stage(nc, ap, scr):
    with ExitStack() as ctx:
        def sb(name, shape, dt=FP32):
            return ctx.enter_context(nc.sbuf_tensor(name, shape, dt))

        def sem(name):
            return ctx.enter_context(nc.semaphore(name))

        x_all = sb("x_all", [P, NTILE, C])
        stats = sb("stats", [P, TPB, 6])
        mean = sb("mean", [P, NTILE])
        mv = sb("mv", [P, TPB, 2])
        var = sb("var", [P, TPB])
        std = sb("std", [P, TPB])
        inv = sb("inv", [P, TPB])
        t1 = sb("t1", [P, TPB])
        t2 = sb("t2", [P, TPB])
        rstd = sb("rstd", [P, NTILE])
        w_attn = sb("w_attn", [P, CB, 2 * C])
        w_k2 = sb("w_k2", [P, CB, C])
        w_ffn = [sb(f"w_ffn{i}", [P, CB, C]) for i in range(3)]
        w_ffn_t = [sb(f"w_ffn_t{i}", [P, CB, C]) for i in range(3)]
        mu = sb("mu", [P, 2, CB])
        eps = sb("eps", [P, 1])
        zrow = sb("zrow", [1, C])
        ident = sb("p_ident", [P, P])
        xn = [sb(f"xn{i}", [P, TPC, C]) for i in range(2)]
        vpad = [sb(f"vpad{i}", [P, TPC, H, PAD]) for i in range(2)]
        xnt = [sb(f"xnt{i}", [P, CB, CH + 1]) for i in range(2)]
        diff = sb("diff", [P, CB, CH])
        xr = sb("xr", [P, CB, CH])
        xk = sb("xk", [P, CB, CH])
        part = sb("part", [P, 4, NS, CH], BF16)
        rest = [sb(f"rest{i}", [P, CH]) for i in range(2)]
        qan = sb("qan", [P, CB, CH])
        ka = sb("ka", [P, TPC, C])
        rgate = sb("rgate", [P, TPC, C])
        apart = sb("apart", [P, 2, CB, NS, CH], BF16)
        arest = [sb(f"arest{i}", [P, CB, CH]) for i in range(2)]
        krelu = sb("krelu", [P, CB, CH])
        kact = sb("kact", [P, CB, CH])
        res = sb("res", [P, TPC, C])
        bank = [ctx.enter_context(nc.psum_tensor(f"pbank{i}", [P, CH], FP32)) for i in range(8)]

        x_loaded = [sem(f"x_loaded{c}") for c in range(CPB)]
        x_rest_loaded = sem("x_rest_loaded")
        w_loaded = sem("w_loaded")
        consts = sem("p_consts")
        zeroed = sem("p_zeroed")
        wt_done = sem("wt_done")
        wt_copied = sem("wt_copied")
        tail_stored = sem("tail_stored")
        loop_sems = []

        def loop_sem(name):
            loop_sems.append(sem(name))
            return loop_sems[-1]

        stat_done = loop_sem("stat_done")
        mv_done = loop_sem("mv_done")
        std_done = loop_sem("std_done")
        chain = loop_sem("rstd_chain")
        xn_done = loop_sem("xn_done")
        vpad_done = loop_sem("vpad_done")
        xt_done = loop_sem("xt_done")
        xnt_copied = loop_sem("xnt_copied")
        edge_done = loop_sem("edge_done")
        diff_done = loop_sem("diff_done")
        mixed = loop_sem("mixed")
        qk_done = loop_sem("qk_done")
        hi_done = loop_sem("hi_done")
        rest_done = loop_sem("rest_done")
        mid_done = loop_sem("mid_done")
        low_done = loop_sem("low_done")
        slope_done = loop_sem("slope_done")
        qan_done = loop_sem("qan_done")
        k2_done = loop_sem("k2_done")
        ka_done = loop_sem("ka_done")
        kat_done = loop_sem("kat_done")
        ahi_done = loop_sem("ahi_done")
        arest_done = loop_sem("arest_done")
        amid_done = loop_sem("amid_done")
        alow_done = loop_sem("alow_done")
        kt_done = loop_sem("kt_done")
        relu_done = loop_sem("relu_done")
        kact_done = loop_sem("kact_done")
        r_done = loop_sem("r_done")
        gate_done = loop_sem("gate_done")
        v_done = loop_sem("v_done")
        rv_done = loop_sem("rv_done")
        res_done = loop_sem("res_done")
        xn_stored = [loop_sem(f"xn_stored{i}") for i in range(2)]
        v_stored = [loop_sem(f"v_stored{i}") for i in range(2)]
        part_stored = loop_sem("part_stored")
        qan_stored = loop_sem("qan_stored")
        ka_stored = loop_sem("ka_stored")
        apart_stored = loop_sem("apart_stored")
        res_stored = loop_sem("res_stored")
        gate = sem("p_gate")
        NC = B * CPB

        x_rows = ap["x"].rearrange("b (n p) c -> p (b n) c", p=P)

        with nc.Block() as block:
            @block.vector
            def _(dve):
                def statistics(b, some):
                    for j in some:
                        i = at(b * TPB + j)
                        nc.vector.bn_stats(stats[:, j, :],
                                           x_all[:, i, :].rearrange("p a c -> p (a c)")).then_inc(stat_done, 1)
                    for j in some:
                        dve.wait_ge(stat_done, START + b * TPB + j + 1)
                        dve.sem_inc(gate, 1)
                        nc.vector.bn_aggr(mv[:, j, :], stats[:, j, :]).then_inc(mv_done, 1)

                def deviation(b):
                    some = at(b * TPB, TPB)
                    dve.wait_ge(mv_done, START + b * TPB + TPB)
                    nc.vector.tensor_scalar(var[:, :], mv[:, :, 1], EPS, None,
                                            ALU.add).then_inc(chain, 1)
                    dve.wait_ge(std_done, START + b + 1)
                    nc.vector.reciprocal(inv[:, :], std[:, :]).then_inc(chain, 1)
                    dve.wait_ge(chain, START + b * 7 + 2)
                    nc.vector.tensor_tensor(t1[:, :], inv[:, :], inv[:, :], ALU.mult).then_inc(chain, 1)
                    dve.wait_ge(chain, START + b * 7 + 3)
                    nc.vector.tensor_tensor(t2[:, :], t1[:, :], var[:, :], ALU.mult).then_inc(chain, 1)
                    dve.wait_ge(chain, START + b * 7 + 4)
                    nc.vector.tensor_scalar(t1[:, :], t2[:, :], -0.5, 1.5, ALU.mult, ALU.add).then_inc(chain, 1)
                    dve.wait_ge(chain, START + b * 7 + 5)
                    nc.vector.tensor_tensor(rstd[:, some], t1[:, :], inv[:, :], ALU.mult).then_inc(chain, 1)
                    nc.vector.tensor_copy(mean[:, some], mv[:, :, 0]).then_inc(chain, 1)
                    dve.wait_ge(chain, START + b * 7 + 7)

                def normalise(c, tile0):
                    for j in range(TPC):
                        i = at(tile0 + j)
                        nc.vector.tensor_scalar(xn[c % 2][:, j, :], x_all[:, i, :].rearrange("p a c -> p (a c)"),
                                                mean[:, i], rstd[:, i],
                                                ALU.subtract, ALU.mult).then_inc(xn_done, 1)

                def batch(b, last):
                    for c in range(CPB):
                        n = b * CPB + c
                        cur, prev = xnt[c % 2], xnt[(c + 1) % 2]
                        dve.wait_ge(xnt_copied, START + n * CB + CB)
                        dve.wait_ge(mixed, START + n * 4)
                        if c == 0:
                            nc.vector.memset(cur[:, :, 0:1], 0.0).then_inc(edge_done, 1)
                        else:
                            nc.vector.tensor_copy(cur[:, :, 0:1], prev[:, :, CH:CH + 1]).then_inc(edge_done, 1)
                        dve.wait_ge(edge_done, START + n + 1)
                        nc.vector.tensor_tensor(diff[:, :, :], cur[:, :, 1:CH + 1], cur[:, :, 0:CH],
                                                ALU.subtract).then_inc(diff_done, 1)
                        dve.wait_ge(diff_done, START + n + 1)
                        for use, dst, free in ((1, xk, kt_done), (0, xr, r_done)):
                            dve.wait_ge(free, START + n * 2)
                            for k in range(CB):
                                nc.vector.scalar_tensor_tensor(
                                    out=dst[:, k, :], in0=diff[:, k, :], scalar=mu[:, use, k:k + 1],
                                    in1=cur[:, k, 0:CH], op0=ALU.mult, op1=ALU.add).then_inc(mixed, 1)
                        for m in range(4):
                            dve.wait_ge(hi_done, START + n * 4 + m + 1)
                            dve.wait_ge(low_done, START + n * 4 + m - 1)
                            if m < CB:
                                dve.wait_ge(slope_done, START + n * 2 + m + 1)
                            nc.vector.tensor_tensor(rest[m % 2][:, :], bank[2 + m][:, :], part[:, m, 0, :],
                                                    ALU.subtract).then_inc(rest_done, 1)
                            if m < CB:
                                nc.vector.scalar_tensor_tensor(out=qan[:, m, :], in0=bank[2 + m][:, :], scalar=-SCALE,
                                                               in1=qan[:, m, :], op0=ALU.mult,
                                                               op1=ALU.max).then_inc(qan_done, 1)
                            if not last:
                                b1 = b + 1
                                if c < CPB - 1:
                                    if c == m == 0:
                                        dve.wait_ge(x_rest_loaded, 16 * (B - 1))
                                    slot, slots = 4 * c + m, 4 * (CPB - 1)
                                    statistics(b1, range(TPB * slot // slots, TPB * (slot + 1) // slots))
                                elif m == 2:
                                    deviation(b1)
                        if not (last and c == CPB - 1):
                            dve.wait_ge(xt_done, START + n * CB)
                            dve.wait_ge(vpad_done, START + n)
                            dve.wait_ge(xn_stored[(c + 1) % 2], START + (b * 2 + (c + 1) // 2) * 16)
                            normalise(c + 1, n * TPC + TPC)
                        dve.wait_ge(ahi_done, START + n * 3 + 1)
                        nc.vector.tensor_tensor(arest[0][:, :, :], qan[:, :, :], apart[:, 0, :, 0, :],
                                                ALU.subtract).then_inc(arest_done, 1)
                        for m in range(CB):
                            dve.wait_ge(ahi_done, START + n * 3 + m + 2)
                            nc.vector.tensor_tensor(arest[1][:, m, :], bank[6 + m][:, :], apart[:, 1, m, 0, :],
                                                    ALU.subtract).then_inc(arest_done, 1)
                        for i in range(2):
                            dve.wait_ge(amid_done, START + n * 2 + i + 1)
                            nc.vector.tensor_tensor(apart[:, i, :, 2, :], arest[i][:, :, :], apart[:, i, :, 1, :],
                                                    ALU.subtract).then_inc(alow_done, 1)
                        dve.wait_ge(res_stored, START + n * 16)
                        for u in range(2):
                            dve.wait_ge(v_done, START + n * 2 + u + 1)
                            dve.wait_ge(gate_done, START + n * 2 + u + 1)
                            gated = rgate[:, 2 * u:2 * u + 2, :].rearrange("p a c -> p (a c)")
                            out = res[:, 2 * u:2 * u + 2, :].rearrange("p a c -> p (a c)")
                            nc.vector.tensor_tensor(out, bank[4 + u][:, :], gated, ALU.mult).then_inc(rv_done, 1)
                            dve.wait_ge(rv_done, START + n * 2 + u + 1)
                            nc.vector.tensor_tensor(
                                out, out, x_all[:, at(n * TPC + 2 * u, 2), :].rearrange("p a c -> p (a c)"),
                                ALU.add).then_inc(res_done, 1)

                for c in range(CPB):
                    dve.wait_ge(x_loaded[c], 16)
                    statistics(0, range(TPC * c, TPC * (c + 1)))
                deviation(0)
                normalise(0, 0)
                dve.wait_ge(w_loaded, 16 * 7)
                with dve.Fori(0, B - 1) as b:
                    batch(b, False)
                batch(B - 1, True)

            @block.tensor
            def _(pe):
                def transpose_chunk(c, n):
                    pe.wait_ge(xn_done, START + n * TPC + TPC)
                    pe.wait_ge(relu_done, START + n * 2)
                    for k in range(CB):
                        for j in range(TPC):
                            last = nc.tensor.transpose(bank[k][:, P * j:P * (j + 1)],
                                                       xn[c % 2][:, j, P * k:P * (k + 1)], ident[:, :])
                        last.then_inc(xt_done, 1)

                def batch(b, last_batch):
                    for c in range(CPB):
                        n = b * CPB + c
                        xt = xnt[c % 2]
                        pe.wait_ge(xnt_copied, START + n * CB + CB)
                        for m in range(4):
                            pe.wait_ge(gate_done if m < 2 else rv_done, START + n * 2)
                            for k in range(CB):
                                last = nc.tensor.matmul(bank[2 + m][:, :], w_attn[:, k, P * m:P * (m + 1)],
                                                        xt[:, k, 1:CH + 1], start=(k == 0), stop=(k == CB - 1))
                            last.then_inc(qk_done, 1)
                        pe.wait_ge(arest_done, START + n * 3)
                        for u in range(2):
                            for j in range(2):
                                t0 = 1 + P * (2 * u + j)
                                for k in range(CB):
                                    last = nc.tensor.matmul(bank[6 + u][:, C * j:C * (j + 1)], xt[:, k, t0:t0 + P],
                                                            w_k2[:, k, :], start=(k == 0), stop=(k == CB - 1))
                            last.then_inc(k2_done, 1)
                        pe.wait_ge(mixed, START + n * 4 + 2)
                        for m in range(CB):
                            for k in range(CB):
                                last = nc.tensor.matmul(bank[m][:, :], w_ffn_t[1][:, k, P * m:P * (m + 1)],
                                                        xk[:, k, :], start=(k == 0), stop=(k == CB - 1))
                            last.then_inc(kt_done, 1)
                        pe.wait_ge(mixed, START + n * 4 + 4)
                        pe.wait_ge(rest_done, START + n * 4 + 2)
                        pe.wait_ge(qan_done, START + n * 2 + 2)
                        for u in range(2):
                            for j in range(2):
                                t0 = P * (2 * u + j)
                                for k in range(CB):
                                    last = nc.tensor.matmul(bank[2 + u][:, C * j:C * (j + 1)], xr[:, k, t0:t0 + P],
                                                            w_ffn_t[0][:, k, :], start=(k == 0), stop=(k == CB - 1))
                            last.then_inc(r_done, 1)
                        pe.wait_ge(ka_done, START + n * 2 + 2)
                        for k in range(CB):
                            for j in range(TPC):
                                last = nc.tensor.transpose(bank[6 + k][:, P * j:P * (j + 1)],
                                                           ka[:, j, P * k:P * (k + 1)], ident[:, :])
                            last.then_inc(kat_done, 1)
                        if not (last_batch and c == CPB - 1):
                            transpose_chunk(c + 1, n + 1)
                        pe.wait_ge(kact_done, START + n * 2 + 2)
                        pe.wait_ge(rest_done, START + n * 4 + 4)
                        for u in range(2):
                            for j in range(2):
                                t0 = P * (2 * u + j)
                                for k in range(CB):
                                    last = nc.tensor.matmul(bank[4 + u][:, C * j:C * (j + 1)], kact[:, k, t0:t0 + P],
                                                            w_ffn_t[2][:, k, :], start=(k == 0), stop=(k == CB - 1))
                            last.then_inc(v_done, 1)

                pe.wait_ge(w_loaded, 16 * 7)
                pe.wait_ge(consts, 7)
                for i in range(3):
                    for k in range(CB):
                        for m in range(CB):
                            last = nc.tensor.transpose(bank[CB * i + k][:, P * m:P * (m + 1)],
                                                       w_ffn[i][:, m, P * k:P * (k + 1)], ident[:, :])
                        last.then_inc(wt_done, 1)
                pe.wait_ge(wt_copied, 6)
                transpose_chunk(0, 0)
                with pe.Fori(0, B - 1) as b:
                    batch(b, False)
                batch(B - 1, True)

            @block.scalar
            def _(act):
                def copy_xnt(c, n):
                    act.wait_ge(mixed, START + n * 4 - 4)
                    act.wait_ge(edge_done, START + n)
                    for k in range(CB):
                        act.wait_ge(xt_done, START + n * CB + k + 1)
                        nc.scalar.activation(xnt[c % 2][:, k, 1:CH + 1], bank[k][:, :],
                                             ACT.Copy).then_inc(xnt_copied, 1)

                def deviation(b):
                    act.wait_ge(mv_done, START + b * TPB + TPB)
                    act.wait_ge(chain, START + b * 7)
                    nc.scalar.activation(std[:, :], mv[:, :, 1],
                                         ACT.Sqrt, bias=eps[:, :]).then_inc(std_done, 1)

                def batch(b, last):
                    for c in range(CPB):
                        n = b * CPB + c
                        act.wait_ge(part_stored, START + n * 16 * 8)
                        act.wait_ge(qan_stored, START + n * 16)
                        act.wait_ge(arest_done, START + n * 3 - 2)
                        for m in range(4):
                            act.wait_ge(qk_done, START + n * 4 + m + 1)
                            nc.scalar.activation(part[:, m, 0, :], bank[2 + m][:, :], ACT.Copy).then_inc(hi_done, 1)
                            if m < CB:
                                nc.scalar.activation(qan[:, m, :], bank[2 + m][:, :], ACT.Copy,
                                                     scale=-SCALE * SLOPE).then_inc(slope_done, 1)
                        if not last and c == CPB - 1:
                            b1 = b + 1
                            deviation(b1)
                        act.wait_ge(ka_stored, START + n * 16)
                        act.wait_ge(kat_done, START + n * 2)
                        for u in range(2):
                            act.wait_ge(k2_done, START + n * 2 + u + 1)
                            nc.scalar.activation(ka[:, 2 * u:2 * u + 2, :].rearrange("p a c -> p (a c)"),
                                                 bank[6 + u][:, :], ACT.Sigmoid,
                                                 scale=MA_K * SCALE).then_inc(ka_done, 1)
                        act.wait_ge(qan_done, START + n * 2 + 2)
                        act.wait_ge(apart_stored, START + n * 16 * 4)
                        nc.scalar.activation(apart[:, 0, :, 0, :], qan[:, :, :], ACT.Copy).then_inc(ahi_done, 1)
                        act.wait_ge(kact_done, START + n * 2)
                        for m in range(CB):
                            act.wait_ge(kt_done, START + n * 2 + m + 1)
                            nc.scalar.activation(krelu[:, m, :], bank[m][:, :], ACT.Relu).then_inc(relu_done, 1)
                        act.wait_ge(v_done, START + n * 2)
                        for m in range(CB):
                            act.wait_ge(relu_done, START + n * 2 + m + 1)
                            nc.scalar.activation(kact[:, m, :], krelu[:, m, :], ACT.Square).then_inc(kact_done, 1)
                        act.wait_ge(rv_done, START + n * 2)
                        for u in range(2):
                            act.wait_ge(r_done, START + n * 2 + u + 1)
                            nc.scalar.activation(rgate[:, 2 * u:2 * u + 2, :].rearrange("p a c -> p (a c)"),
                                                 bank[2 + u][:, :], ACT.Sigmoid).then_inc(gate_done, 1)
                        for m in range(CB):
                            act.wait_ge(kat_done, START + n * 2 + m + 1)
                            nc.scalar.activation(apart[:, 1, m, 0, :], bank[6 + m][:, :],
                                                 ACT.Copy).then_inc(ahi_done, 1)
                        if not (last and c == CPB - 1):
                            copy_xnt(c + 1, n + 1)
                        for i in range(2):
                            act.wait_ge(arest_done, START + n * 3 + 2 * i + 1)
                            nc.scalar.activation(apart[:, i, :, 1, :], arest[i][:, :, :],
                                                 ACT.Copy).then_inc(amid_done, 1)

                act.dma_start(w_attn[:, :, :], ap["w_attn"].rearrange("(k p) n -> p k n", p=P)).then_inc(w_loaded, 16)
                act.dma_start(w_k2[:, :, :], ap["w_k2"].rearrange("(k p) n -> p k n", p=P)).then_inc(w_loaded, 16)
                for i, name in enumerate(("w_r", "w_k", "w_v")):
                    act.dma_start(w_ffn[i][:, :, :],
                                  ap[name].rearrange("(k p) n -> p k n", p=P)).then_inc(w_loaded, 16)
                with nc.allow_non_contiguous_dma(reason="256 mixing weights, one per partition"):
                    for i, name in enumerate(("mu_r", "mu_k")):
                        act.dma_start(mu[:, i, :], ap[name].rearrange("(k p) -> p k", p=P)).then_inc(w_loaded, 16)
                for i in range(3):
                    for k in range(CB):
                        act.wait_ge(wt_done, CB * i + k + 1)
                        nc.scalar.activation(w_ffn_t[i][:, k, :], bank[CB * i + k][:, 0:C],
                                             ACT.Copy).then_inc(wt_copied, 1)
                act.wait_ge(consts, 7)
                deviation(0)
                copy_xnt(0, 0)
                with act.Fori(0, B - 1) as b:
                    batch(b, False)
                batch(B - 1, True)

            @block.gpsimd
            def _(pool):
                nc.gpsimd.memset(zrow[:, :], 0.0).then_inc(zeroed, 1)
                nc.gpsimd.memset(ident[:, :], 0.0).then_inc(consts, 1)
                nc.gpsimd.memset(eps[:, :], EPS).then_inc(consts, 1)
                for i in range(2):
                    nc.gpsimd.memset(vpad[i][:, :, :, :], 0.0).then_inc(consts, 1)
                pool.wait_ge(consts, 4)
                nc.gpsimd.affine_select(out=ident[:, :], in_=ident[:, :], compare_op=ALU.not_equal, fill=1.0,
                                        base=0, pattern=[[-1, P]], channel_multiplier=1).then_inc(consts, 1)
                for i in range(2):
                    nc.gpsimd.memset(vpad[i][:, :, :, D:D + 1], 1.0).then_inc(consts, 1)
                pool.wait_ge(consts, 7)
                with pool.Fori(0, B) as b:
                    for c in range(CPB):
                        n = b * CPB + c
                        pool.wait_ge(xn_done, START + n * TPC + TPC)
                        pool.wait_ge(v_stored[c % 2], START + (b * 2 + c // 2) * 16 * QPB)
                        pool.sem_inc(gate, 1)
                        nc.gpsimd.tensor_copy(vpad[c % 2][:, :, :, 0:D].rearrange("p j h d -> p (j h) d"),
                                              xn[c % 2][:, :, :].rearrange("p j (h d) -> p (j h) d", d=D)
                                              ).then_inc(vpad_done, 1)
                        pool.wait_ge(part_stored, START + n * 16 * 8)
                        for m in range(4):
                            pool.wait_ge(rest_done, START + n * 4 + m + 1)
                            pool.sem_inc(gate, 1)
                            nc.gpsimd.tensor_copy(part[:, m, 1, :], rest[m % 2][:, :]).then_inc(mid_done, 1)
                            pool.wait_ge(mid_done, START + n * 4 + m + 1)
                            nc.gpsimd.tensor_tensor(part[:, m, 2, :], rest[m % 2][:, :], part[:, m, 1, :],
                                                    ALU.subtract).then_inc(low_done, 1)

            @block.sync
            def _(sp):
                def rows(dram, n):
                    return dram[at(n * CH, CH), :].rearrange("(j p) c -> p j c", p=P)

                for c in range(CPB):
                    tiles = slice(TPC * c, TPC * (c + 1))
                    sp.dma_start(x_all[:, tiles, :], x_rows[:, tiles, :]).then_inc(x_loaded[c], 16)
                for s in loop_sems:
                    sp.sem_inc(s, START)
                sp.wait_ge(w_loaded, 16 * 7)
                for b in range(1, B):
                    tiles = slice(TPB * b, TPB * (b + 1))
                    sp.dma_start(x_all[:, tiles, :], x_rows[:, tiles, :]).then_inc(x_rest_loaded, 16)
                sp.wait_ge(zeroed, 1)
                sp.dma_start(scr.xn[B * T:B * T + 1, :], zrow[:, :]).then_inc(tail_stored, 16)
                with sp.Fori(0, B) as b:
                    for c in range(CPB):
                        n = b * CPB + c
                        ts = slice(CH * c, CH * (c + 1))
                        sp.wait_ge(xn_done, START + n * TPC + TPC)
                        sp.dma_start(rows(scr.xn, n), xn[c % 2][:, :, :]).then_inc(xn_stored[c % 2], 16)
                        sp.wait_ge(vpad_done, START + n + 1)
                        for qd in range(QPB):
                            sp.dma_start(scr.v[at(b * QPB + qd), ts, :].rearrange("a (j p) w -> p (a j) w", p=P),
                                         vpad[c % 2][:, :, QH * qd:QH * (qd + 1), :].rearrange("p j h w -> p j (h w)")
                                         ).then_inc(v_stored[c % 2], 16)
                        sp.wait_ge(qan_done, START + n * 2 + 2)
                        sp.dma_start(scr.qa[at(b), :, :, ts].rearrange("a k p t -> p (a k) t"),
                                     qan[:, :, :]).then_inc(qan_stored, 16)
                        for m in range(4):
                            sp.wait_ge(low_done, START + n * 4 + m + 1)
                            dst = scr.q if m < 2 else scr.k
                            for half in range(2):
                                sp.dma_start(
                                    dst[at(b * QPB + 2 * (m % 2) + half), :, :, ts].rearrange("a s r t -> (a r) s t"),
                                    part[64 * half:64 * half + 64, m, :, :]).then_inc(part_stored, 16)
                        sp.wait_ge(ka_done, START + n * 2 + 2)
                        sp.dma_start(rows(scr.ka, n), ka[:, :, :]).then_inc(ka_stored, 16)
                        for i, dst in enumerate((scr.qa_part, scr.ka_part)):
                            sp.wait_ge(alow_done, START + n * 2 + i + 1)
                            for m in range(CB):
                                sp.dma_start(dst[at(b), :, P * m:P * (m + 1), ts].rearrange("a s r t -> (a r) s t"),
                                             apart[:, i, m, :, :]).then_inc(apart_stored, 16)
                        sp.wait_ge(res_done, START + n * 2 + 2)
                        sp.dma_start(rows(scr.res, n), res[:, :, :]).then_inc(res_stored, 16)
                sp.wait_ge(tail_stored, 16)
                for i in range(2):
                    sp.wait_ge(xn_stored[i], START + NC // 2 * 16)
                    sp.wait_ge(v_stored[i], START + NC // 2 * 16 * QPB)
                sp.wait_ge(part_stored, START + NC * 16 * 8)
                sp.wait_ge(qan_stored, START + NC * 16)
                sp.wait_ge(apart_stored, START + NC * 16 * 4)
                sp.wait_ge(ka_stored, START + NC * 16)
                sp.wait_ge(res_stored, START + NC * 16)


class MixInputs:
    TILES = 2
    FIRST = 1 + 2 * len(Q_PARTS)
    THEN = 4

    def __init__(self, nc, ctx, scr, b):
        W = self.TILES * P

        def sb(name, shape, dt=FP32):
            return ctx.enter_context(nc.sbuf_tensor(f"{name}{b}", shape, dt))

        self.scr, self.b = scr, b
        self.kst = sb("m_kst", [P, H, W], BF16)
        self.qst = sb("m_qst", [P, H, W], BF16)
        self.yraw = sb("yraw", [P, QPB, W])
        self.vnext = sb("vnext", [P, self.TILES, C])
        self.qa = sb("qa", [P, CB, W])
        self.ka = sb("ka_rows", [P, self.TILES, C])
        self.res = sb("mres", [P, self.TILES, C])
        self.loaded = ctx.enter_context(nc.semaphore(f"parts_loaded{b}"))
        self.rest_loaded = ctx.enter_context(nc.semaphore(f"rest_loaded{b}"))

    def columns(self, r):
        return at(r * (self.TILES * P), self.TILES * P)

    def load(self, sp, r):
        b, scr = self.b, self.scr
        for dst, parts, src in ((self.kst, K_PARTS, scr.ka_part), (self.qst, Q_PARTS, scr.qa_part)):
            for i, part in enumerate(parts):
                sp.dma_start(dst[D * i:D * (i + 1), :, :],
                             src[b, part, :, self.columns(r)].rearrange("(h d) t -> d h t", d=D)
                             ).then_inc(self.loaded, 16)
        sp.dma_start(self.yraw[:, :, :],
                     scr.y[QPB * b:QPB * (b + 1), :, self.columns(r)].rearrange("q p t -> p q t")
                     ).then_inc(self.loaded, 16)

    def load_rest(self, sp, r):
        scr = self.scr
        row = r * (self.TILES * P) + self.b * T

        def tokens(dram, first):
            return dram[at(first, self.TILES * P), :].rearrange("(i p) c -> p i c", p=P)

        sp.dma_start(self.vnext[:, :, :], tokens(scr.xn, row + 1)).then_inc(self.rest_loaded, 16)
        sp.dma_start(self.qa[:, :, :], scr.qa[self.b, :, :, self.columns(r)].rearrange("k p t -> p k t")
                     ).then_inc(self.rest_loaded, 16)
        sp.dma_start(self.ka[:, :, :], tokens(scr.ka, row)).then_inc(self.rest_loaded, 16)
        sp.dma_start(self.res[:, :, :], tokens(scr.res, row)).then_inc(self.rest_loaded, 16)


def attention_stage(nc, ap, scr, ahead, w_proj, w_loaded):
    NK = T // P
    BUFS = 3
    SLOTS = 3
    PAIRS = 3
    RQ = 6
    VQ = 2
    SEGS = CPB
    LOWEST = -3.0e38
    units = [(i, h, seg) for i in range(NK) for h in range(QH) for seg in range(i // TPC + 1)]
    NU = len(units) + 1
    blocks = [(c, j) for c in range(CPB) for j in range(TPC * (c + 1))]
    NB = len(blocks)
    EARLY = QH * TPC
    assert BUFS * NU % SLOTS == 0 and BUFS * NB % PAIRS == 0 and (NQ - 1) % BUFS == 0

    def cut(c, j):
        return max(0, P * (j - TPC * c))

    def width(u):
        i, _, seg = u
        return min(CH, P * (i + 1) - CH * seg)

    LAST = NB - TPC - 1
    OVERHEAD = 240
    UNIT_OVERHEAD = 64
    turn_at = LAST + 2

    def spread(some, first, last):
        cost = [sum(CH - cut(*blk) + OVERHEAD for blk in blocks[first:n + 1]) for n in range(first, last + 1)]
        ucost = [sum(width(u) + UNIT_OVERHEAD for u in some[:n + 1]) for n in range(len(some))]
        return [sum(uc * cost[-1] <= ucost[-1] * co for uc in ucost) for co in cost]

    quota = spread(units[EARLY:], 0, LAST)
    early_quota = spread(units[:EARLY], turn_at, NB - 1)

    with ExitStack() as ctx:
        def sb(name, shape, dt=FP32):
            return ctx.enter_context(nc.sbuf_tensor(name, shape, dt))

        def sem(name):
            return ctx.enter_context(nc.semaphore(name))

        qst = [sb(f"qst{i}", [P, QH, T], BF16) for i in range(BUFS)]
        kst = [sb(f"kst{i}", [P, QH, T], BF16) for i in range(BUFS)]
        val = [sb(f"val{i}", [P, NK, QH * PAD]) for i in range(BUFS)]
        prob = [sb(f"prob{i}", [P, 2, CH]) for i in range(2 * PAIRS)]
        yt = [sb(f"yt{i}", [P, CH]) for i in range(2)]
        pmax = sb("pmax", [P, NK * QH, SEGS])
        nmax = sb("nmax", [P, NK * QH])
        nrest = sb("nrest", [P, NK * QH])
        npart = sb("npart", [P, NS, NK * QH], BF16)
        mrow = sb("mrow", [NK * QH, NS, P], BF16)
        ident = sb("a_ident", [P, P], BF16)
        mask_kq = sb("mask_kq", [P, P], BF16)
        mask_qk = sb("mask_qk", [P, CH])
        sums = [sb(f"sums{i}", [P, CH], BF16) for i in range(SLOTS)]
        score = [ctx.enter_context(nc.psum_tensor(f"score{i}", [P, 2, CH], FP32)) for i in range(2)]
        acc = ctx.enter_context(nc.psum_tensor("acc", [P, CH], FP32))
        slot = [ctx.enter_context(nc.psum_tensor(f"slot{i}", [P, CH], FP32)) for i in range(SLOTS)]

        consts = sem("a_consts")
        first_loaded = sem("a_first_loaded")
        ones_done = sem("a_ones")
        loop_sems = []

        def loop_sem(name):
            loop_sems.append(sem(name))
            return loop_sems[-1]

        q_loaded = [loop_sem(f"q_loaded{i}") for i in range(BUFS)]
        v_loaded = [loop_sem(f"v_loaded{i}") for i in range(BUFS)]
        m_loaded = [loop_sem(f"m_loaded{i}") for i in range(BUFS)]
        peak_scored = loop_sem("peak_scored")
        peak_read = loop_sem("peak_read")
        nmax_done = loop_sem("nmax_done")
        scored = loop_sem("scored")
        exp_done = loop_sem("exp_done")
        pv_done = loop_sem("pv_done")
        acc_copied = loop_sem("acc_copied")
        gate = sem("a_gate")
        y_stored = [loop_sem(f"y_stored{i}") for i in range(2)]

        def steps(eng, step):
            R = (NQ - 1) // BUFS
            step(0, 0, True, False)
            with eng.Fori(0, R - 1) as r:
                for s in range(1, BUFS + 1):
                    step(r, s, True, True)
            for s in range(1, BUFS + 1):
                step(R - 1, s, True, True)
            step(R, 1, False, True)

        def has_next(r, s):
            return not isinstance(r, int) or r * BUFS + s < NQ - 1

        def filled(r, s):
            return r + s // BUFS + 1

        with nc.Block() as block:
            @block.sync
            def _(sp):
                def load_parts(n, buf, tokens, loaded):
                    for dst, parts, src in ((qst[buf], Q_PARTS, scr.q), (kst[buf], K_PARTS, scr.k)):
                        for i, part in enumerate(parts):
                            sp.dma_start(dst[D * i:D * (i + 1), :, tokens],
                                         src[at(n), part, :, tokens].rearrange("a (h d) t -> d (a h) t", d=D)
                                         ).then_inc(loaded, 16)

                def load_values(n, buf):
                    for i in range(VQ):
                        some = slice(NK // VQ * i, NK // VQ * (i + 1))
                        sp.dma_start(val[buf][:, some, :],
                                     scr.v[at(n), :, :].rearrange("a (j p) w -> p (a j) w", p=P)[:, some, :]
                                     ).then_inc(v_loaded[buf], 16)

                def store(n, c):
                    sp.wait_ge(acc_copied, START + (n - 1) * CPB + c + 1)
                    sp.dma_start(scr.y[at(n - 1), :, CH * c:CH * (c + 1)].rearrange("a p t -> (a p) t"),
                                 yt[c % 2][:, :]).then_inc(y_stored[c % 2], 16)

                def rows(n, buf):
                    sp.wait_ge(peak_read, START + n * NU + NU)
                    for i in range(NS):
                        sp.dma_start(qst[buf][SR + i:SR + i + 1, :, :].rearrange("a h (i t) -> a (h i) t", t=P),
                                     mrow[:, i, :]).then_inc(m_loaded[buf], 16)

                def step(r, s, more):
                    n = r * BUFS + s
                    sp.wait_ge(pv_done, START + (n - 1) * NB)
                    if more:
                        load_parts(n + 1, (s + 1) % BUFS, slice(0, T), q_loaded[(s + 1) % BUFS])
                        load_values(n + 1, (s + 1) % BUFS)
                    for c in range(CPB - 1):
                        store(n, c)
                    rows(n, s % BUFS)
                    store(n, CPB - 1)

                for s in loop_sems:
                    sp.sem_inc(s, START)
                load_parts(0, 0, slice(0, T // 2), first_loaded)
                load_parts(0, 0, slice(T // 2, T), q_loaded[0])
                load_values(0, 0)
                load_parts(1, 1, slice(0, T), q_loaded[1])
                load_values(1, 1)
                rows(0, 0)
                with sp.Fori(0, (NQ - 1) // BUFS - 1) as r:
                    for s in range(1, BUFS + 1):
                        step(r, s, True)
                for s in range(1, BUFS + 1):
                    step((NQ - 1) // BUFS - 1, s, s < BUFS)
                ahead.load(sp, 0)
                ahead.load_rest(sp, 0)
                sp.dma_start(w_proj[:, :, :], ap["w_proj"].rearrange("(k p) n -> p k n", p=P)).then_inc(w_loaded, 16)
                for c in range(CPB):
                    store(NQ, c)
                for i in range(2):
                    sp.wait_ge(y_stored[i], START + NQ * CPB // 2 * 16)

            @block.tensor
            def _(pe):
                def peak(r, s, w):
                    n = r * BUFS + s
                    buf, dst = s % BUFS, slot[(NU * s + w) % SLOTS]
                    i, h, seg = units[w]
                    wd = width(units[w])
                    pe.wait_ge(peak_read, START + n * NU + w - SLOTS + 1)
                    nc.tensor.matmul(dst[:, 0:wd], qst[buf][0:SR, h, P * i:P * (i + 1)],
                                     kst[buf][0:SR, h, CH * seg:CH * seg + wd], start=True, stop=True
                                     ).then_inc(peak_scored, 1)

                def turn(r, s):
                    n = r * BUFS + s
                    dst = slot[(NU * s + NU - 1) % SLOTS][:, :].bitcast(BF16)
                    pe.wait_ge(peak_read, START + n * NU + NU - SLOTS)
                    pe.wait_ge(nmax_done, START + n * 5 + 5)
                    pe.sem_inc(gate, 1)
                    for i in range(NS):
                        last = nc.tensor.transpose(dst[0:NK * QH, P * i:P * (i + 1)], npart[:, i, :], ident[:, :])
                    last.then_inc(peak_scored, 1)

                def scores(r, s, b, half):
                    m = r * BUFS + s - 1
                    c, j = blocks[b]
                    q, k, dst = qst[(s - 1) % BUFS], kst[(s - 1) % BUFS], score[half]
                    t0 = CH * c + cut(c, j)
                    wd = CH - cut(c, j)
                    diag = j >= TPC * c
                    pe.wait_ge(exp_done, START + m * 2 * NB + 2 * b + half - 1)
                    for e in range(2):
                        h = 2 * half + e
                        last = nc.tensor.matmul(dst[:, e, 0:wd], k[0:MR, h, P * j:P * (j + 1)],
                                                q[0:MR, h, t0:t0 + wd], start=True, stop=not diag)
                        if diag:
                            last = nc.tensor.matmul(dst[:, e, 0:P], ident[:, :], mask_kq[:, :],
                                                    start=False, stop=True)
                    last.then_inc(scored, 1)

                def product(r, s, b):
                    m = r * BUFS + s - 1
                    c, j = blocks[b]
                    v = val[(s - 1) % BUFS]
                    wd = CH - cut(c, j)
                    pe.wait_ge(exp_done, START + m * 2 * NB + 2 * b + 2)
                    if j == 0:
                        pe.wait_ge(acc_copied, START + m * CPB + c)
                    for h in range(QH):
                        p = prob[(2 * (NB * (s - 1) + b) + h // 2) % (2 * PAIRS)]
                        last = nc.tensor.matmul(acc[PAD * h:PAD * (h + 1), cut(c, j):CH],
                                                v[:, j, PAD * h:PAD * (h + 1)], p[:, h % 2, 0:wd],
                                                start=(j == 0), stop=(j == TPC * (c + 1) - 1))
                    last.then_inc(pv_done, 1)

                def step(r, s, peaks, main):
                    if not main:
                        pe.wait_ge(consts, 7)
                        pe.wait_ge(first_loaded, 16 * 2 * RQ)
                        for w in range(len(units)):
                            if units[w] == (NK // 2, 0, 0):
                                pe.wait_ge(q_loaded[s % BUFS], START + 16 * 2 * RQ * filled(r, s))
                            peak(r, s, w)
                        turn(r, s)
                        for w in range(EARLY):
                            if w == 0:
                                pe.wait_ge(q_loaded[s + 1], START + 16 * 2 * RQ * filled(r, s + 1))
                            peak(r, s + 1, w)
                        return
                    pe.wait_ge(ones_done, BUFS)
                    pe.wait_ge(m_loaded[(s - 1) % BUFS], START + 16 * NS * filled(r, s - 1))
                    pe.wait_ge(v_loaded[(s - 1) % BUFS], START + 16 * VQ * filled(r, s - 1))
                    done, early = EARLY, 0
                    for b in range(NB):
                        todo = []
                        if peaks and b <= LAST:
                            todo = [(s, w) for w in range(done, EARLY + quota[b])]
                            done = EARLY + quota[b]
                        elif peaks and b >= turn_at and has_next(r, s):
                            if b == turn_at:
                                pe.wait_ge(q_loaded[(s + 1) % BUFS], START + 16 * 2 * RQ * filled(r, s + 1))
                            todo = [(s + 1, w) for w in range(early, early_quota[b - turn_at])]
                            early = early_quota[b - turn_at]
                        gap = [len(todo) // 3 + (len(todo) % 3 > x) for x in range(3)]
                        for x in range(3):
                            if x < 2:
                                scores(r, s, b, x)
                            elif b > 0:
                                product(r, s, b - 1)
                            if peaks and b == turn_at and x == 0:
                                turn(r, s)
                            for _ in range(gap[x]):
                                peak(r, *todo.pop(0))
                    product(r, s, NB - 1)

                steps(pe, step)

            @block.gpsimd
            def _(pool):
                nc.gpsimd.memset(ident[:, :], 0.0).then_inc(consts, 1)
                nc.gpsimd.memset(mask_qk[:, :], 0.0).then_inc(consts, 1)
                nc.gpsimd.memset(mask_kq[:, :], 0.0).then_inc(consts, 1)
                pool.wait_ge(consts, 4)
                nc.gpsimd.affine_select(out=ident[:, :], in_=ident[:, :], compare_op=ALU.not_equal, fill=1.0,
                                        base=0, pattern=[[-1, P]], channel_multiplier=1).then_inc(consts, 1)
                own = mask_qk[:, CH - P:CH]
                nc.gpsimd.affine_select(out=own, in_=own, compare_op=ALU.is_ge, fill=MASKED,
                                        base=0, pattern=[[-1, P]], channel_multiplier=1).then_inc(consts, 1)
                nc.gpsimd.affine_select(out=mask_kq[:, :], in_=mask_kq[:, :], compare_op=ALU.is_ge, fill=MASKED,
                                        base=0, pattern=[[1, P]], channel_multiplier=-1).then_inc(consts, 1)
                pool.wait_ge(consts, 7)
                for i in range(BUFS):
                    if i:
                        pool.wait_ge(ones_done, i)
                    nc.gpsimd.memset(kst[i][SR:MR, :, :], 1.0).then_inc(ones_done, 1)

            @block.scalar
            def _(act):
                def step(r, s, peaks, main):
                    if not main:
                        return
                    m = r * BUFS + s - 1
                    for b, (c, j) in enumerate(blocks):
                        wd = CH - cut(c, j)
                        act.wait_ge(pv_done, START + m * NB + b - PAIRS + 1)
                        for half in range(2):
                            p = prob[(2 * (NB * (s - 1) + b) + half) % (2 * PAIRS)]
                            act.wait_ge(scored, START + m * 2 * NB + 2 * b + half + 1)
                            nc.scalar.activation(p[:, :, 0:wd], score[half][:, :, 0:wd], ACT.Exp,
                                                 scale=SCALE).then_inc(exp_done, 1)
                        if c and j == 0:
                            copy_sums(m, c - 1, b)
                    copy_sums(m, CPB - 1, NB)

                def copy_sums(m, c, products):
                    act.wait_ge(pv_done, START + m * NB + products)
                    act.wait_ge(y_stored[c % 2], START + (m * (CPB // 2) + c // 2) * 16)
                    nc.scalar.activation(yt[c % 2][:, :], acc[:, :], ACT.Copy).then_inc(acc_copied, 1)

                steps(act, step)

            @block.vector
            def _(dve):
                def reduce(r, s, w):
                    n = r * BUFS + s
                    i, h, seg = units[w]
                    dve.wait_ge(peak_scored, START + n * NU + w + 1)
                    if w == 0:
                        dve.wait_ge(nmax_done, START + n * 5)
                    wd = width(units[w])
                    src, dst = slot[(NU * s + w) % SLOTS][:, 0:wd], pmax[:, NK * h + i, seg:seg + 1]
                    if seg == i // TPC:
                        dve.sem_inc(gate, 1)
                        nc.vector.tensor_tensor_reduce(out=sums[(NU * s + w) % SLOTS][:, 0:wd], in0=src,
                                                       in1=mask_qk[:, CH - wd:CH],
                                                       scale=1.0, scalar=LOWEST, op0=ALU.add, op1=ALU.max,
                                                       accum_out=dst).then_inc(peak_read, 1)
                    else:
                        nc.vector.tensor_reduce(dst, src, AX.X, ALU.max).then_inc(peak_read, 1)

                def step(r, s, peaks, main):
                    if not peaks:
                        return
                    n = r * BUFS + s
                    for w in range(EARLY if main else 0, len(units)):
                        reduce(r, s, w)
                    dve.wait_ge(peak_read, START + n * NU + NU - 1)
                    nc.vector.tensor_reduce(nmax[:, :], pmax[:, :, :], AX.X, ALU.max, negate=True
                                            ).then_inc(nmax_done, 1)
                    dve.wait_ge(nmax_done, START + n * 5 + 1)
                    nc.vector.tensor_copy(npart[:, 0, :], nmax[:, :]).then_inc(nmax_done, 1)
                    dve.wait_ge(nmax_done, START + n * 5 + 2)
                    nc.vector.tensor_tensor(nrest[:, :], nmax[:, :], npart[:, 0, :], ALU.subtract
                                            ).then_inc(nmax_done, 1)
                    dve.wait_ge(nmax_done, START + n * 5 + 3)
                    nc.vector.tensor_copy(npart[:, 1, :], nrest[:, :]).then_inc(nmax_done, 1)
                    dve.wait_ge(nmax_done, START + n * 5 + 4)
                    nc.vector.tensor_tensor(npart[:, 2, :], nrest[:, :], npart[:, 1, :], ALU.subtract
                                            ).then_inc(nmax_done, 1)
                    dve.wait_ge(peak_scored, START + n * NU + NU)
                    back = (s - 1) % BUFS
                    fills = r + (s - 1) // BUFS + 1
                    dve.wait_ge(m_loaded[back], START + 16 * NS * fills)
                    nc.vector.tensor_copy(mrow[:, :, :].rearrange("p s t -> p (s t)"),
                                          slot[(NU * s + NU - 1) % SLOTS][:, :].bitcast(BF16)[0:NK * QH, 0:NS * P]
                                          ).then_inc(peak_read, 1)
                    if has_next(r, s):
                        for w in range(EARLY):
                            reduce(r, s + 1, w)

                nc.vector.memset(pmax[:, :, :], LOWEST).then_inc(consts, 1)
                dve.wait_ge(consts, 7)
                steps(dve, step)


def mix_stage(nc, ap, scr, ahead, w_proj, w_loaded):
    TILES = MixInputs.TILES
    NI = TILES * B
    STEPS = TPB // TILES
    OUTS = 4
    GH = P // D
    items = [(2 * half + one, t) for half in range(B // 2) for t in range(TILES) for one in range(2)]
    closes = [t == TILES - 1 for _, t in items]
    FIRST, THEN = MixInputs.FIRST, MixInputs.THEN
    with ExitStack() as ctx:
        def sb(name, shape, dt=FP32):
            return ctx.enter_context(nc.sbuf_tensor(name, shape, dt))

        def sem(name):
            return ctx.enter_context(nc.semaphore(name))

        ident = sb("m_ident", [P, P])
        strict = sb("strict", [P, P])
        own = sb("own", [P, H])
        inputs = [ahead] + [MixInputs(nc, ctx, scr, b) for b in range(1, B)]
        kst, qst = [x.kst for x in inputs], [x.qst for x in inputs]
        yraw, vnext = [x.yraw for x in inputs], [x.vnext for x in inputs]
        qa, ka, res = [x.qa for x in inputs], [x.ka for x in inputs], [x.res for x in inputs]
        state = [sb(f"state{i}", [P, C]) for i in range(B)]
        den = [sb(f"den{i}", [P, H]) for i in range(2)]
        y = [sb(f"y{i}", [P, H, D]) for i in range(2)]
        e = [sb(f"e{i}", [P, H, PAD]) for i in range(2)]
        am = [sb(f"am{i}", [P, QPB, QH, P]) for i in range(2)]
        snew = [sb(f"snew{i}", [P, C]) for i in range(2)]
        y2t = [sb(f"y2t{i}", [P, QPB * P]) for i in range(2)]
        yi = [sb(f"yi{i}", [P, H, D]) for i in range(2)]
        ysum = [sb(f"ysum{i}", [P, H, D]) for i in range(2)]
        ysumt = [sb(f"ysumt{i}", [P, CB, P]) for i in range(2)]
        outt = [sb(f"outt{i}", [P, C]) for i in range(OUTS)]
        abank = [ctx.enter_context(nc.psum_tensor(f"abank{i}", [P, QH, P], FP32)) for i in range(QPB)]
        ybank = ctx.enter_context(nc.psum_tensor("ybank", [P, CH], FP32))
        zbank = ctx.enter_context(nc.psum_tensor("zbank", [P, CH], FP32))
        obank = ctx.enter_context(nc.psum_tensor("obank", [P, QPB, P], FP32))
        kbank = ctx.enter_context(nc.psum_tensor("kbank", [P, CH], FP32))

        consts = sem("m_consts")
        gate = sem("m_gate")
        loop_sems = []

        def loop_sem(name):
            loop_sems.append(sem(name))
            return loop_sems[-1]

        loaded, rest_loaded = [x.loaded for x in inputs], [x.rest_loaded for x in inputs]
        loop_sems += loaded + rest_loaded
        yt_done = loop_sem("m_yt")
        den_done = loop_sem("m_den")
        y_done = loop_sem("m_y")
        e_done = loop_sem("m_e")
        a_done = loop_sem("m_a")
        am_done = loop_sem("m_am")
        i_done = loop_sem("m_i")
        yi_done = loop_sem("m_yi")
        o_done = loop_sem("m_o")
        y2t_done = loop_sem("m_y2t")
        s_done = loop_sem("m_s")
        snew_done = loop_sem("m_snew")
        state_done = loop_sem("m_state")
        z_done = loop_sem("m_z")
        ysum_done = loop_sem("m_ysum")
        w_done = loop_sem("m_w")
        ysumt_done = loop_sem("m_ysumt")
        p_done = loop_sem("m_p")
        out_done = loop_sem("m_out")
        stored = [loop_sem(f"m_stored{i}") for i in range(OUTS)]
        CONSTS = 5 + 4 + B

        with nc.Block() as block:
            @block.sync
            def _(sp):
                def store(r, k):
                    m = r * NI + k
                    b, t = items[k]
                    row = (r * TILES + t) * P
                    sp.wait_ge(out_done, START + m + 1)
                    sp.dma_start(ap["out"][b, at(row, P), :], outt[k % OUTS][:, :]
                                 ).then_inc(stored[k % OUTS], 16)

                def step(r, first, last):
                    for k in range(NI):
                        m = r * NI + k
                        if closes[k] and not last:
                            sp.wait_ge(a_done, START + m * QPB + QPB)
                            sp.sem_inc(gate, 1)
                            sp.wait_ge(yt_done, START + m + 1)
                            sp.sem_inc(gate, 1)
                            inputs[items[k][0]].load(sp, r + 1)
                        if not (first and k < 2):
                            r0, k0 = r + (k - 2) // NI, (k - 2) % NI
                            store(r0, k0)
                            if closes[k0] and not (last and k >= 2):
                                inputs[items[k0][0]].load_rest(sp, r0 + 1)

                for s in loop_sems:
                    sp.sem_inc(s, START)
                for b in range(1, B):
                    inputs[b].load(sp, 0)
                    inputs[b].load_rest(sp, 0)
                step(0, True, False)
                with sp.Fori(1, STEPS - 1) as r:
                    step(r, False, False)
                step(STEPS - 1, False, True)
                for k in (NI - 2, NI - 1):
                    store(STEPS - 1, k)
                for i in range(OUTS):
                    sp.wait_ge(stored[i], START + STEPS * NI // OUTS * 16)

            @block.tensor
            def _(pe):
                def span(k):
                    t = items[k][1]
                    return slice(P * t, P * (t + 1))

                def turn(r, k):
                    m = r * NI + k
                    b = items[k][0]
                    pe.wait_ge(loaded[b], START + r * (16 * FIRST) + 16 * FIRST)
                    pe.wait_ge(out_done, START + m - 2)
                    for q in range(QPB):
                        last = nc.tensor.transpose(ybank[:, P * q:P * (q + 1)], yraw[b][:, q, span(k)], ident[:, :])
                    last.then_inc(yt_done, 1)

                def inner(r, k):
                    m = r * NI + k
                    pe.wait_ge(loaded[items[k][0]], START + r * (16 * FIRST) + 16 * FIRST)
                    for a in range(QPB):
                        pe.wait_ge(am_done, START + m * QPB - QPB + a + 1)
                        for j in range(QH):
                            last = nc.tensor.matmul(abank[a][:, j, :], kst[items[k][0]][0:SR, QH * a + j, span(k)],
                                                    qst[items[k][0]][0:SR, QH * a + j, span(k)], start=True, stop=True)
                        last.then_inc(a_done, 1)

                def carried(r, k):
                    m = r * NI + k
                    b, t = items[k]
                    pe.wait_ge(rest_loaded[b], START + r * (16 * THEN) + 16 * THEN)
                    before = 2 if t else NI - 2 * (TILES - 1)
                    pe.wait_ge(state_done, START + m - before + 1)
                    pe.wait_ge(yi_done, START + m)
                    pe.wait_ge(snew_done, START + m)
                    for g in range(CB):
                        last = nc.tensor.matmul(kbank[:, P * g:P * (g + 1)], qa[items[k][0]][:, g, span(k)],
                                                state[items[k][0]][:, P * g:P * (g + 1)], start=True, stop=True)
                    last.then_inc(i_done, 1)

                def apply(r, k):
                    m = r * NI + k
                    pe.wait_ge(y2t_done, START + m)
                    pe.wait_ge(e_done, START + m + 1)
                    pe.wait_ge(am_done, START + m * QPB + QPB)
                    for a in range(QPB):
                        for j in range(QH):
                            last = nc.tensor.matmul(obank[PAD * j:PAD * (j + 1), a, :], e[k % 2][:, QH * a + j, :],
                                                    am[k % 2][:, a, j, :], start=True, stop=True)
                    last.then_inc(o_done, 1)

                def turn_back(r, k):
                    m = r * NI + k
                    pe.wait_ge(y2t_done, START + m + 1)
                    pe.wait_ge(ysumt_done, START + m)
                    for q in range(QPB):
                        last = nc.tensor.transpose(zbank[:, P * q:P * (q + 1)], y2t[k % 2][:, P * q:P * (q + 1)],
                                                   ident[:, :])
                    last.then_inc(z_done, 1)

                def update(r, k):
                    m = r * NI + k
                    pe.wait_ge(yi_done, START + m + 1)
                    for g in range(CB):
                        last = nc.tensor.matmul(kbank[:, C + P * g:C + P * (g + 1)],
                                                ka[items[k][0]][:, items[k][1], P * g:P * (g + 1)],
                                                e[k % 2][:, GH * g:GH * (g + 1), 0:D], start=True, stop=True)
                    last.then_inc(s_done, 1)

                def turn_sum(r, k):
                    m = r * NI + k
                    pe.wait_ge(ysum_done, START + m + 1)
                    for g in range(CB):
                        last = nc.tensor.transpose(
                            zbank[:, P * g:P * (g + 1)],
                            ysum[k % 2][:, GH * g:GH * (g + 1), :].rearrange("p h d -> p (h d)"), ident[:, :])
                    last.then_inc(w_done, 1)

                def project(r, k, ahead):
                    m = r * NI + k
                    pe.wait_ge(ysumt_done, START + m + 1)
                    pe.wait_ge(y_done, START + m + 1 + ahead)
                    pe.wait_ge(out_done, START + m)
                    for g in range(CB):
                        last = nc.tensor.matmul(ybank[:, 0:C], ysumt[k % 2][:, g, :], w_proj[:, g, :],
                                                start=(g == 0), stop=(g == CB - 1))
                    last.then_inc(p_done, 1)

                def step(r, first, last):
                    for k in range(NI):
                        after = not (last and k == NI - 1)
                        before = not (first and k == 0)
                        r1, k1 = r + (k + 1) // NI, (k + 1) % NI
                        r0, k0 = r + (k - 1) // NI, (k - 1) % NI
                        if after:
                            inner(r1, k1)
                        carried(r, k)
                        apply(r, k)
                        if after:
                            turn(r1, k1)
                        if before:
                            turn_sum(r0, k0)
                        update(r, k)
                        turn_back(r, k)
                        if before:
                            project(r0, k0, 1 + after)

                pe.wait_ge(consts, CONSTS)
                pe.wait_ge(w_loaded, 16)
                turn(0, 0)
                inner(0, 0)
                step(0, True, False)
                with pe.Fori(1, STEPS - 1) as r:
                    step(r, False, False)
                step(STEPS - 1, False, True)
                turn_sum(STEPS - 1, NI - 1)
                project(STEPS - 1, NI - 1, 0)

            @block.gpsimd
            def _(pool):
                nc.gpsimd.memset(ident[:, :], 0.0).then_inc(consts, 1)
                nc.gpsimd.memset(strict[:, :], 1.0).then_inc(consts, 1)
                nc.gpsimd.memset(own[:, :], 1.0).then_inc(consts, 1)
                for i in range(2):
                    nc.gpsimd.memset(e[i][:, :, :], 0.0).then_inc(consts, 1)
                pool.wait_ge(consts, 5)
                nc.gpsimd.affine_select(out=ident[:, :], in_=ident[:, :], compare_op=ALU.not_equal, fill=1.0,
                                        base=0, pattern=[[-1, P]], channel_multiplier=1).then_inc(consts, 1)
                nc.gpsimd.affine_select(out=strict[:, :], in_=strict[:, :], compare_op=ALU.is_gt, fill=0.0,
                                        base=0, pattern=[[1, P]], channel_multiplier=-1).then_inc(consts, 1)
                rows = own[:, :].rearrange("p (g h) -> p g h", g=CB)
                nc.gpsimd.affine_select(out=rows, in_=rows, compare_op=ALU.is_ge, fill=0.0,
                                        base=0, pattern=[[0, CB], [-D, GH]], channel_multiplier=1).then_inc(consts, 1)
                pool.wait_ge(consts, 8)
                nc.gpsimd.affine_select(out=rows, in_=rows, compare_op=ALU.is_ge, fill=0.0,
                                        base=D - 1, pattern=[[0, CB], [D, GH]],
                                        channel_multiplier=-1).then_inc(consts, 1)
                for b in range(B):
                    nc.gpsimd.memset(state[b][:, :], 0.0).then_inc(consts, 1)

                def error(r, k):
                    m = r * NI + k
                    pool.wait_ge(rest_loaded[items[k][0]], START + r * (16 * THEN) + 16 * THEN)
                    pool.wait_ge(y_done, START + m + 1)
                    pool.wait_ge(s_done, START + m - 1)
                    nc.gpsimd.tensor_tensor(e[k % 2][:, :, 0:D], y[k % 2][:, :, :],
                                            vnext[items[k][0]][:, items[k][1], :].rearrange("p (h d) -> p h d", d=D),
                                            ALU.subtract).then_inc(e_done, 1)

                def keep(r, k):
                    m = r * NI + k
                    pool.wait_ge(i_done, START + m + 1)
                    pool.wait_ge(snew_done, START + m + 1)
                    nc.gpsimd.tensor_tensor(state[items[k][0]][:, :], state[items[k][0]][:, :], snew[k % 2][:, :],
                                            ALU.add).then_inc(state_done, 1)

                pool.wait_ge(consts, CONSTS)
                error(0, 0)
                with pool.Fori(0, STEPS - 1) as r:
                    for k in range(NI):
                        error(r + (k + 1) // NI, (k + 1) % NI)
                        keep(r, k)
                for k in range(NI):
                    if k < NI - 1:
                        error(STEPS - 1, k + 1)
                    keep(STEPS - 1, k)

            @block.scalar
            def _(act):
                def back(r, k):
                    m = r * NI + k
                    act.wait_ge(o_done, START + m + 1)
                    act.wait_ge(z_done, START + m - 1)
                    nc.scalar.activation(y2t[k % 2][:, :], obank[:, :, :].rearrange("p q t -> p (q t)"),
                                         ACT.Copy).then_inc(y2t_done, 1)

                def both(r, k):
                    m = r * NI + k
                    act.wait_ge(w_done, START + m + 1)
                    act.wait_ge(p_done, START + m - 1)
                    nc.scalar.activation(ysumt[k % 2][:, :, :].rearrange("p g t -> p (g t)"), zbank[:, 0:C],
                                         ACT.Copy).then_inc(ysumt_done, 1)

                def step(r, first):
                    for k in range(NI):
                        back(r, k)
                        if not (first and k == 0):
                            both(r + (k - 1) // NI, (k - 1) % NI)

                step(0, True)
                with act.Fori(1, STEPS) as r:
                    step(r, False)
                both(STEPS - 1, NI - 1)

            @block.vector
            def _(dve):
                def attention(r, k):
                    m = r * NI + k
                    dve.wait_ge(yt_done, START + m + 1)
                    sums = ybank[:, :].rearrange("p (h w) -> p h w", w=PAD)
                    nc.vector.reciprocal(den[k % 2][:, :], sums[:, :, D]).then_inc(den_done, 1)
                    dve.wait_ge(den_done, START + m + 1)
                    dve.wait_ge(yi_done, START + m - 1)
                    dve.wait_ge(e_done, START + m - 1)
                    nc.vector.tensor_tensor(y[k % 2][:, :, :], sums[:, :, 0:D],
                                            den[k % 2][:, :].unsqueeze(2).to_broadcast([P, H, D]),
                                            ALU.mult).then_inc(y_done, 1)

                def masks(r, k, some):
                    m = r * NI + k
                    dve.wait_ge(o_done, START + m - 1)
                    for a in some:
                        dve.wait_ge(a_done, START + m * QPB + a + 1)
                        nc.vector.tensor_tensor(am[k % 2][:, a, :, :], abank[a][:, :, :],
                                                strict[:, :].unsqueeze(1).to_broadcast([P, QH, P]),
                                                ALU.mult).then_inc(am_done, 1)

                def carried(r, k):
                    m = r * NI + k
                    dve.wait_ge(i_done, START + m + 1)
                    dve.wait_ge(y_done, START + m + 1)
                    dve.wait_ge(ysum_done, START + m - 1)
                    nc.vector.tensor_tensor(yi[k % 2][:, :, :], kbank[:, 0:C].rearrange("p (h d) -> p h d", d=D),
                                            y[k % 2][:, :, :], ALU.add).then_inc(yi_done, 1)

                def total(r, k):
                    m = r * NI + k
                    dve.wait_ge(z_done, START + m + 1)
                    dve.wait_ge(yi_done, START + m + 1)
                    dve.wait_ge(w_done, START + m - 1)
                    nc.vector.tensor_tensor(ysum[k % 2][:, :, :],
                                            zbank[:, :].rearrange("p (h w) -> p h w", w=PAD)[:, :, 0:D],
                                            yi[k % 2][:, :, :], ALU.add).then_inc(ysum_done, 1)

                def own_blocks(r, k):
                    m = r * NI + k
                    dve.wait_ge(s_done, START + m + 1)
                    dve.wait_ge(state_done, START + m - 1)
                    nc.vector.tensor_tensor(snew[k % 2][:, :].rearrange("p (h d) -> p h d", d=D),
                                            kbank[:, C:2 * C].rearrange("p (h d) -> p h d", d=D),
                                            own[:, :].unsqueeze(2).to_broadcast([P, H, D]),
                                            ALU.mult).then_inc(snew_done, 1)

                def finish(r, k):
                    m = r * NI + k
                    dve.wait_ge(p_done, START + m + 1)
                    dve.wait_ge(stored[k % OUTS], START + (r * (NI // OUTS) + k // OUTS) * 16)
                    nc.vector.tensor_tensor(outt[k % OUTS][:, :], ybank[:, 0:C], res[items[k][0]][:, items[k][1], :],
                                            ALU.add).then_inc(out_done, 1)

                def step(r, first, last):
                    for k in range(NI):
                        r1, k1 = r + (k + 1) // NI, (k + 1) % NI
                        after = not (last and k == NI - 1)
                        if after:
                            masks(r1, k1, range(QPB // 2))
                        carried(r, k)
                        if after:
                            masks(r1, k1, range(QPB // 2, QPB))
                            attention(r1, k1)
                        own_blocks(r, k)
                        total(r, k)
                        if not (first and k == 0):
                            finish(r + (k - 1) // NI, (k - 1) % NI)

                dve.wait_ge(consts, CONSTS)
                attention(0, 0)
                masks(0, 0, range(QPB))
                step(0, True, False)
                with dve.Fori(1, STEPS - 1) as r:
                    step(r, False, False)
                step(STEPS - 1, False, True)
                finish(STEPS - 1, NI - 1)


def build(nc, x, w_attn, w_k2, w_proj, w_r, w_k, w_v, mu_r, mu_k, out):
    ap = dict(x=x, w_attn=w_attn, w_k2=w_k2, w_proj=w_proj, w_r=w_r, w_k=w_k, w_v=w_v,
              mu_r=mu_r, mu_k=mu_k, out=out)
    scr = Scratch(nc)
    project_stage(nc, ap, scr)
    with ExitStack() as ctx:
        ahead = MixInputs(nc, ctx, scr, 0)
        w_proj = ctx.enter_context(nc.sbuf_tensor("w_proj", [P, CB, C], FP32))
        w_loaded = ctx.enter_context(nc.semaphore("m_w_loaded"))
        attention_stage(nc, ap, scr, ahead, w_proj, w_loaded)
        mix_stage(nc, ap, scr, ahead, w_proj, w_loaded)


_INS = ['L0_attn_x', 'L0_attn_W_attn', 'L0_attn_W_k2', 'L0_attn_W_proj', 'L0_ffn_W_r', 'L0_ffn_W_k',
        'L0_ffn_W_v', 'L0_ffn_mu_r', 'L0_ffn_mu_k']
_OUTS = [((B, T, C), 'float32')]


def kernel(**inputs):
    import numpy as _np
    import concourse.bacc as _bacc
    from concourse import mybir as _mybir
    from concourse.bass_utils import run_bass_kernel_spmd as _run

    nc = _bacc.Bacc("TRN2", target_bir_lowering=False, num_devices=1)
    arrays, args = {}, []
    for name in _INS:
        a = _np.ascontiguousarray(inputs[name])
        arrays[f"in_{name}_dram"] = a
        args.append(nc.dram_tensor(f"in_{name}_dram", a.shape, _mybir.dt.from_np(a.dtype), kind="ExternalInput").ap())
    for i, (shape, dtype) in enumerate(_OUTS):
        dt = _mybir.dt.from_np(_np.dtype(dtype))
        args.append(nc.dram_tensor(f"out_{i}_dram", shape, dt, kind="ExternalOutput").ap())
    build(nc, *args)
    r = _run(nc, [arrays], core_ids=[0])
    got = tuple(r.results[0][f"out_{i}_dram"] for i in range(len(_OUTS)))
    return got[0]
```
